# Optimizing a Trainium2 kernel written in Bass

```python
import numpy as np
import jax
import jax.numpy as jnp

def _softmax(x, axis=-1):
    return jax.nn.softmax(x, axis=axis)

def _gelu(x):
    return jax.nn.gelu(x, approximate=True)

def _silu(x):
    return jax.nn.silu(x)

def _sigmoid(x):
    return jax.nn.sigmoid(x)

def _layernorm(x, axis=-1, eps=1e-05):
    m = jnp.mean(x, axis=axis, keepdims=True)
    v = jnp.var(x, axis=axis, keepdims=True)
    return (x - m) / jnp.sqrt(v + eps)

def _scatter_add(tgt, idx, src, axis=0):
    return tgt.at[idx].add(src)

def _segment_sum(src, seg, n):
    return jax.ops.segment_sum(src, seg, n)
kernel_name = 'mk_macaron_d1_jaxref_r4_743593'

def setup_inputs(seed: int=0):
    np.random.seed(seed)
    _w = jnp.asarray

    def _L0_attn_setup():
        import jax, jax.numpy as jnp
        import numpy as np
        B, N, D, H = (4, 1024, 256, 16)
        HD = D // H
        MLP = 4 * D

        def _ln(x, w, b):
            m = x.mean(-1, keepdims=True)
            v = x.var(-1, keepdims=True)
            return (x - m) / jnp.sqrt(v + 1e-05) * w + b
        key = jax.random.key(seed)
        ks = jax.random.split(key, 12)
        s = 1.0 / np.sqrt(D)
        sm = 1.0 / np.sqrt(MLP)
        return {'q_x': jax.random.normal(ks[0], (B, N, D), jnp.float32), 'ln1_w': jnp.ones((D,), jnp.float32), 'ln1_b': jnp.zeros((D,), jnp.float32), 'wq': jax.random.normal(ks[1], (D, D), jnp.float32) * s, 'bq': jnp.zeros((D,), jnp.float32), 'wk': jax.random.normal(ks[2], (D, D), jnp.float32) * s, 'bk': jnp.zeros((D,), jnp.float32), 'wv': jax.random.normal(ks[3], (D, D), jnp.float32) * s, 'bv': jnp.zeros((D,), jnp.float32), 'wo': jax.random.normal(ks[4], (D, D), jnp.float32) * s, 'bo': jnp.zeros((D,), jnp.float32), 'ln2_w': jnp.ones((D,), jnp.float32), 'ln2_b': jnp.zeros((D,), jnp.float32), 'fc_w': jax.random.normal(ks[5], (D, MLP), jnp.float32) * s, 'fc_b': jnp.zeros((MLP,), jnp.float32), 'proj_w': jax.random.normal(ks[6], (MLP, D), jnp.float32) * sm, 'proj_b': jnp.zeros((D,), jnp.float32)}
    _L0_attn_in = _L0_attn_setup()

    def _L0_ffn_setup():
        import jax, jax.numpy as jnp
        import numpy as np
        D_MODEL = 256
        EXPERT_DIM = 1024
        N_EXPERTS = 8
        CAP_FACTOR = 0.5
        key = jax.random.key(seed)
        ks = jax.random.split(key, 7)
        inp = {'input': jax.random.normal(ks[0], (4, 1024, D_MODEL), dtype=jnp.float32), 'w_switch': jax.random.normal(ks[1], (D_MODEL, N_EXPERTS), dtype=jnp.float32) * 0.02, 'b_switch': jnp.zeros((N_EXPERTS,), jnp.float32), 'w1': jax.random.normal(ks[2], (N_EXPERTS, D_MODEL, EXPERT_DIM), dtype=jnp.float32) * 0.02, 'b1': jnp.zeros((N_EXPERTS, EXPERT_DIM), jnp.float32), 'w2': jax.random.normal(ks[3], (N_EXPERTS, EXPERT_DIM, D_MODEL), dtype=jnp.float32) * 0.02, 'b2': jnp.zeros((N_EXPERTS, D_MODEL), jnp.float32)}
        return inp
    _L0_ffn_in = _L0_ffn_setup()
    _d = {'L0_attn_q_x': _L0_attn_in['q_x'], 'L0_attn_ln1_w': _L0_attn_in['ln1_w'], 'L0_attn_ln1_b': _L0_attn_in['ln1_b'], 'L0_attn_wq': _L0_attn_in['wq'], 'L0_attn_bq': _L0_attn_in['bq'], 'L0_attn_wk': _L0_attn_in['wk'], 'L0_attn_bk': _L0_attn_in['bk'], 'L0_attn_wv': _L0_attn_in['wv'], 'L0_attn_bv': _L0_attn_in['bv'], 'L0_attn_wo': _L0_attn_in['wo'], 'L0_attn_bo': _L0_attn_in['bo'], 'L0_attn_ln2_w': _L0_attn_in['ln2_w'], 'L0_attn_ln2_b': _L0_attn_in['ln2_b'], 'L0_attn_fc_w': _L0_attn_in['fc_w'], 'L0_attn_fc_b': _L0_attn_in['fc_b'], 'L0_attn_proj_w': _L0_attn_in['proj_w'], 'L0_attn_proj_b': _L0_attn_in['proj_b'], 'L0_ffn_w_switch': _L0_ffn_in['w_switch'], 'L0_ffn_b_switch': _L0_ffn_in['b_switch'], 'L0_ffn_w1': _L0_ffn_in['w1'], 'L0_ffn_b1': _L0_ffn_in['b1'], 'L0_ffn_w2': _L0_ffn_in['w2'], 'L0_ffn_b2': _L0_ffn_in['b2']}
    _x0 = _d['L0_attn_q_x']
    _d['L0_attn_q_x'] = jax.random.normal(jax.random.fold_in(jax.random.key(seed), 1), (8, 512, 256), dtype=_x0.dtype)
    del _x0
    return _d

def reference(L0_attn_q_x, L0_attn_ln1_w, L0_attn_ln1_b, L0_attn_wq, L0_attn_bq, L0_attn_wk, L0_attn_bk, L0_attn_wv, L0_attn_bv, L0_attn_wo, L0_attn_bo, L0_attn_ln2_w, L0_attn_ln2_b, L0_attn_fc_w, L0_attn_fc_b, L0_attn_proj_w, L0_attn_proj_b, L0_ffn_w_switch, L0_ffn_b_switch, L0_ffn_w1, L0_ffn_b1, L0_ffn_w2, L0_ffn_b2):

    def _L0_attn_ref(q_x, ln1_w, ln1_b, wq, bq, wk, bk, wv, bv, wo, bo, ln2_w, ln2_b, fc_w, fc_b, proj_w, proj_b):
        import jax, jax.numpy as jnp
        import numpy as np
        B, N, D, H = (4, 1024, 256, 16)
        HD = D // H
        MLP = 4 * D

        def _ln(x, w, b):
            m = x.mean(-1, keepdims=True)
            v = x.var(-1, keepdims=True)
            return (x - m) / jnp.sqrt(v + 1e-05) * w + b
        b, n, c = q_x.shape
        xn = _ln(q_x, ln1_w, ln1_b)
        q = (xn @ wq + bq).reshape(b, n, H, HD).transpose(0, 2, 1, 3)
        k = (xn @ wk + bk).reshape(b, n, H, HD).transpose(0, 2, 1, 3)
        v = (xn @ wv + bv).reshape(b, n, H, HD).transpose(0, 2, 1, 3)
        fq = jax.nn.elu(q) + 1.0
        fk = jax.nn.elu(k) + 1.0
        kv = jnp.einsum('bhnd,bhne->bnde', fk, v)
        qkv = jnp.einsum('bhnd,bnde->bhne', fq, kv)
        k_sum = fk.sum(axis=1)
        qk = jnp.einsum('bhnd,bnd->bhn', fq, k_sum)
        attn = qkv / (qk[..., None] + 1e-06)
        attn = attn.transpose(0, 2, 1, 3).reshape(b, n, c)
        attn = attn @ wo + bo
        x = q_x + attn
        h = _ln(x, ln2_w, ln2_b)
        h = jax.nn.gelu(h @ fc_w + fc_b, approximate=False)
        return x + (h @ proj_w + proj_b)

    def _L0_ffn_ref(input, w_switch, b_switch, w1, b1, w2, b2):
        import jax, jax.numpy as jnp
        import numpy as np
        D_MODEL = 256
        EXPERT_DIM = 1024
        N_EXPERTS = 8
        CAP_FACTOR = 0.5
        B, S, D = input.shape
        T = B * S
        E = b_switch.shape[0]
        capacity = int(CAP_FACTOR * T / E)
        x = input.reshape(T, D)
        logits = x @ w_switch + b_switch
        probs = jax.nn.softmax(logits, axis=-1)
        pmax = probs.max(axis=-1)
        routes = probs.argmax(axis=-1)
        oh = (routes[:, None] == jnp.arange(E)[None, :]).astype(jnp.int32)
        pos = (jnp.cumsum(oh, axis=0) * oh).sum(-1) - 1
        keep = pos < capacity
        slot = jnp.where(keep, routes * capacity + pos, E * capacity)
        buf = jnp.zeros((E * capacity + 1, D), x.dtype).at[slot].set(x)
        buf_e = buf[:E * capacity].reshape(E, capacity, D)
        h = jax.nn.relu(jnp.einsum('ecd,edh->ech', buf_e, w1) + b1[:, None, :])
        y = jnp.einsum('ech,ehd->ecd', h, w2) + b2[:, None, :]
        y_flat = jnp.concatenate([y.reshape(E * capacity, D), jnp.zeros((1, D), x.dtype)], axis=0)
        out = jnp.where(keep[:, None], y_flat[slot], x)
        scale = pmax / jax.lax.stop_gradient(pmax)
        out = out * scale[:, None]
        return out.reshape(B, S, D)
    x = L0_attn_q_x
    x = x + 0.5 * _L0_ffn_ref(_layernorm(x, axis=-1), L0_ffn_w_switch, L0_ffn_b_switch, L0_ffn_w1, L0_ffn_b1, L0_ffn_w2, L0_ffn_b2)
    x = x + _L0_attn_ref(_layernorm(x, axis=-1), L0_attn_ln1_w, L0_attn_ln1_b, L0_attn_wq, L0_attn_bq, L0_attn_wk, L0_attn_bk, L0_attn_wv, L0_attn_bv, L0_attn_wo, L0_attn_bo, L0_attn_ln2_w, L0_attn_ln2_b, L0_attn_fc_w, L0_attn_fc_b, L0_attn_proj_w, L0_attn_proj_b)
    x = x + 0.5 * _L0_ffn_ref(_layernorm(x, axis=-1), L0_ffn_w_switch, L0_ffn_b_switch, L0_ffn_w1, L0_ffn_b1, L0_ffn_w2, L0_ffn_b2)
    return x

_drawn_inputs = setup_inputs


def setup_inputs(seed=0):
    import zlib

    import numpy as np

    out = dict(_drawn_inputs(seed))
    spreads = {'L0_attn_ln1_w': (1.0, 0.2),
     'L0_attn_ln1_b': (0.0, 0.391),
     'L0_attn_bq': (0.0, 0.8),
     'L0_attn_bk': (0.0, 0.8),
     'L0_attn_bv': (0.0, 0.384),
     'L0_attn_bo': (0.0, 0.1),
     'L0_attn_ln2_w': (1.0, 0.2),
     'L0_attn_ln2_b': (0.0, 0.1),
     'L0_attn_fc_b': (0.0, 0.1),
     'L0_attn_proj_b': (0.0, 0.1),
     'L0_ffn_b_switch': (0.0, 0.1),
     'L0_ffn_b1': (0.0, 0.304),
     'L0_ffn_b2': (0.0, 0.1)}
    factors = {'L0_attn_wq': 2.758}
    for name, (base, spread) in spreads.items():
        noise = np.random.default_rng([zlib.crc32(name.encode()), seed]).standard_normal(out[name].shape)
        drawn = base * np.exp(spread * noise) if base else spread * noise
        out[name] = jnp.asarray(drawn.astype(out[name].dtype))
    for name, factor in factors.items():
        out[name] = (out[name] * factor).astype(out[name].dtype)
    return out
```

```python
from contextlib import ExitStack

import concourse.bass as bass
from concourse import mybir

F32 = mybir.dt.float32
F32R = mybir.dt.float32r
BF16 = mybir.dt.bfloat16
I32 = mybir.dt.int32
ALU = mybir.AluOpType
ACT = mybir.ActivationFunctionType
AX = mybir.AxisListType.X

P = 128
GROUP = 4
EPS = 1e-5
ATTN_EPS = 1e-6
CAP_FACTOR = 0.5


class Stream:

    def __init__(self, sem):
        self.sem, self.count, self.queue, self.seen = sem, 0, [], {}

    def _waits(self, after):
        need = {}
        for event in after:
            if event is not None:
                sem, value = event
                if self.seen.get(id(sem), 0) < value:
                    self.seen[id(sem)] = value
                    need[id(sem)] = (sem, value)
        for sem, value in need.values():
            self.queue.append(lambda eng, sem=sem, value=value: eng.wait_ge(sem, value))

    def do(self, instruction, *after):
        self._waits(after)
        self.count += 1
        self.queue.append(lambda eng: instruction(eng).then_inc(self.sem, 1))
        return self.sem, self.count

    def quiet(self, instruction, *after):
        self._waits(after)
        self.queue.append(instruction)

    def dma(self, ring, transfer, *after):
        sem, value, before = ring.next()
        self._waits((*after, before))
        self.queue.append(lambda eng: transfer(eng).then_inc(sem, 16))
        return sem, value

    def wait(self, *after):
        self._waits(after)

    def play(self, eng):
        for step in self.queue:
            step(eng)


class Ring:

    def __init__(self, sems):
        self.sems, self.values, self.used = sems, [0] * len(sems), 0

    def next(self):
        i = self.used % len(self.sems)
        before = (self.sems[i], self.values[i]) if self.values[i] else None
        self.values[i] += 16
        self.used += 1
        return self.sems[i], self.values[i], before

    def all(self):
        return [(s, v) for s, v in zip(self.sems, self.values) if v]


def build(nc, x_in, ln1_w, ln1_b, wq, bq, wk, bk, wv, bv, wo, bo, ln2_w, ln2_b,
          fc_w, fc_b, proj_w, proj_b, w_switch, b_switch, w1, b1, w2, b2, out):
    B, N, D = x_in.shape
    T = B * N
    NT = T // P
    NG = NT // GROUP
    KD = D // P
    HEADS = 16
    HD = D // HEADS
    HID = fc_w.shape[1]
    KM = HID // P
    E = b_switch.shape[0]
    CAP = int(CAP_FACTOR * T / E)
    SLOTS = E * CAP
    ST = CAP // P
    EH = w1.shape[2]
    KE = EH // P
    ROW = 2 * D + 2
    ID_COL, SC_COL = 2 * D, 2 * D + 1
    GT = GROUP * P
    NOWHERE = 1 << 16
    assert KD == 2 and HEADS * HD == D and KE % 2 == 0 and ST == 2

    x_rows = x_in.rearrange("b n d -> (b n) d")
    out_rows = out.rearrange("b n d -> (b n) d")
    slots_dram = [nc.dram_tensor(f"slots{i}", [SLOTS, ROW], F32).ap() for i in range(2)]
    mid_rows = nc.dram_tensor("mid_rows", [T, D], F32).ap()

    with ExitStack() as ctx:
        def sem(name):
            return ctx.enter_context(nc.semaphore(name))

        def ring(name, n):
            return Ring([sem(f"{name}{i}") for i in range(n)])

        pe, dve, act, pool, sp = (Stream(sem(f"s_{n}")) for n in ("pe", "dve", "act", "pool", "sp"))
        rings = []

        def new_ring(name, n):
            rings.append(ring(name, n))
            return rings[-1]

        r_const = new_ring("d_const", 8)
        r_weight = new_ring("d_weight", 4)
        r_x = new_ring("d_x", 8)
        r_rows = new_ring("d_rows", 4)
        r_store = new_ring("d_store", 8)
        r_scatter = new_ring("d_scatter", 12)
        r_final = new_ring("d_final", 4)

        def tile(stack, name, shape, dt=F32):
            return stack.enter_context(nc.sbuf_tensor(name, shape, dt))

        bank = [ctx.enter_context(nc.psum_tensor(f"bank{i}", [P, 512], F32)) for i in range(8)]

        ident = tile(ctx, "ident", [P, P])
        upto = tile(ctx, "upto", [P, P], BF16)
        ones_bf = tile(ctx, "ones_bf", [P, P], BF16)
        ones_row = tile(ctx, "ones_row", [1, P])
        ones_two = tile(ctx, "ones_two", [2, P], F32R)
        token_id = tile(ctx, "token_id", [P, NT], I32)
        expert_i = tile(ctx, "expert_i", [P, 2, GROUP, E], I32)
        expert_f = tile(ctx, "expert_f", [P, 2, GROUP, E])
        slot_base, first_wins = expert_f[:, 0], expert_f[:, 1]
        switch_w = tile(ctx, "switch_w", [P, KD, E])
        switch_b = tile(ctx, "switch_b", [1, E])
        col_rows = E * KE + KM + 4 * KD
        cols = tile(ctx, "cols", [P, col_rows])
        C_FCB = E * KE
        C_LN = C_FCB + KM
        BO, PB = 3 * D, 4 * D
        bias_rows = tile(ctx, "bias_rows", [2, 5 * D], F32R)
        seen_sum = tile(ctx, "seen_sum", [P, 2, E], BF16)
        minus_half = tile(ctx, "minus_half", [P, 1])
        e_mh = pool.do(lambda e: e.memset(minus_half[:], -0.5))

        qkv_w = [tile(ctx, f"qkv_w{i}", [P, KD, 3 * D], F32R) for i in range(2)]
        o_w = [tile(ctx, f"o_w{i}", [P, KD, D], F32R) for i in range(2)]
        up_w = [tile(ctx, f"up_w{i}", [P, KD, HID], F32R) for i in range(2)]
        down_w = [tile(ctx, f"down_w{i}", [P, KM, D], F32R) for i in range(2)]

        def f32(ap):
            return ap.bitcast(F32)

        def product(dst, left, right, first, last, *after, signal=True):
            (lh, ll), (rh, rl) = left, right
            pe.quiet(lambda e: e.matmul(dst, lh, rh, start=first, stop=False, skip_group_check=True), *after)
            pe.quiet(lambda e: e.matmul(dst, lh, rl, start=False, stop=False, skip_group_check=True))
            go = pe.do if signal else pe.quiet
            return go(lambda e: e.matmul(dst, ll, rh, start=False, stop=last, skip_group_check=True))

        def add_bias(dst, rows, first, *after):
            pe.quiet(lambda e: e.matmul(dst, ones_two[:, 0:P], rows, start=first, stop=False,
                                        skip_group_check=True), *after)

        def turn(dst, src, *after, start=True, stop=True, signal=True):
            go = pe.do if signal else pe.quiet
            return go(lambda e: e.matmul(dst, src, ident[:], is_transpose=True, start=start, stop=stop,
                                         skip_group_check=True), *after)

        with ExitStack() as once:
            raw = tile(once, "raw", [P, KM * D])
            raw2 = tile(once, "raw2", [P, KM * D])
            col_src = tile(once, "col_src", [col_rows, P])
            bias_raw = tile(once, "bias_raw", [1, 5 * D])
            bias_low = tile(once, "bias_low", [1, 5 * D], F32R)
            blank = tile(once, "blank", [P, ROW])
            e_ident0 = pool.do(lambda e: e.memset(ident[:], 0.0))
            e_upto0 = pool.do(lambda e: e.memset(upto[:], 1.0))
            e_ident = pool.do(lambda e: e.affine_select(
                out=ident[:], in_=ident[:], compare_op=ALU.not_equal, fill=1.0, base=0,
                pattern=[[-1, P]], channel_multiplier=1), e_ident0)
            e_upto = pool.do(lambda e: e.affine_select(
                out=upto[:], in_=upto[:], compare_op=ALU.is_ge, fill=0.0, base=0,
                pattern=[[1, P]], channel_multiplier=-1), e_upto0)
            e_blank0 = pool.do(lambda e: e.memset(blank[:], 0.0))
            e_blank = pool.do(lambda e: e.memset(blank[:, ID_COL:ID_COL + 1].bitcast(I32), NOWHERE), e_blank0)
            e_ids = pool.do(lambda e: e.iota(token_id[:], pattern=[[P, NT]], base=0, channel_multiplier=1))
            pool.do(lambda e: e.iota(expert_i[:, 0], pattern=[[0, GROUP], [CAP, E]], base=0, channel_multiplier=0))
            e_iota = pool.do(lambda e: e.iota(expert_i[:, 1], pattern=[[0, GROUP], [-1, E]], base=E,
                                              channel_multiplier=0))
            e_ones = dve.do(lambda e: e.memset(ones_bf[:], 1.0))
            dve.do(lambda e: e.memset(ones_row[:], 1.0))
            dve.do(lambda e: e.memset(f32(ones_two[:]), 1.0))
            dve.do(lambda e: e.memset(seen_sum[:], 0.0))
            e_consts = dve.do(lambda e: e.tensor_copy(expert_f[:], expert_i[:]), e_iota)

            e_blank_rows = [sp.dma(r_store, lambda e, s=s: e.dma_start(
                s.rearrange("(c p) r -> p c r", p=P),
                blank[:].unsqueeze(1).broadcast_to([P, SLOTS // P, ROW])), e_blank) for s in slots_dram]

            e_sw = sp.dma(r_const, lambda e: e.dma_start(switch_w[:], w_switch.rearrange("(k p) e -> p k e", p=P)))
            e_sb = sp.dma(r_const, lambda e: e.dma_start(switch_b[:], b_switch.unsqueeze(0)))
            col_parts = [(b1.rearrange("e (m p) -> (e m) p", p=P), E * KE), (fc_b.rearrange("(m p) -> m p", p=P), KM)]
            col_parts += [(v.rearrange("(m p) -> m p", p=P), KD) for v in (ln1_w, ln1_b, ln2_w, ln2_b)]
            e_cols, at = [], 0
            for src, n in col_parts:
                e_cols.append(sp.dma(r_const, lambda e, src=src, at=at, n=n: e.dma_start(col_src[at:at + n, :], src)))
                at += n
            e_brow = [sp.dma(r_const, lambda e, v=v, i=i: e.dma_start(bias_raw[:, i * D:(i + 1) * D], v.unsqueeze(0)))
                      for i, v in enumerate((bq, bk, bv, bo, proj_b))]
            e = turn(bank[0][:, 0:col_rows], col_src[:], e_ident, *e_cols) if col_rows == P else pe.do(
                lambda e: e.matmul(bank[0][:, 0:col_rows], col_src[:], ident[0:col_rows, 0:col_rows],
                                   is_transpose=True, start=True, stop=True), e_ident, *e_cols)
            e_cols_t = dve.do(lambda e: e.tensor_copy(cols[:], bank[0][:, 0:col_rows]), e)

            e = dve.do(lambda e: e.tensor_copy(bias_rows[0:1, :], bias_raw[:]), *e_brow)
            e = dve.do(lambda e: e.tensor_tensor(bias_low[:], bias_raw[:], f32(bias_rows[0:1, :]), ALU.subtract), e)
            e_bias = sp.dma(r_const, lambda e: e.dma_start(f32(bias_rows[1:2, :]), f32(bias_low[:])), e)

            e_mid_w = []
            raws = [raw, raw2]
            free = [None, None]
            loads = [
                (qkv_w, [(wq, 0, D), (wk, D, D), (wv, 2 * D, D)], 3 * D, KD),
                (o_w, [(wo, 0, D)], D, KD),
                (up_w, [(fc_w, 0, HID)], HID, KD),
                (down_w, [(proj_w, 0, D)], D, KM),
            ]
            for i, (dst, parts, width, k) in enumerate(loads):
                buf = raws[i % 2][:, 0:k * width].rearrange("p (k n) -> p k n", k=k)
                got = [sp.dma(r_weight, lambda e, w=w, c=c, n=n, buf=buf: e.dma_start(
                    buf[:, :, c:c + n], w.rearrange("(k p) n -> p k n", p=P)), free[i % 2]) for w, c, n in parts]
                e = act.do(lambda e, dst=dst, buf=buf: e.copy(dst[0][:], buf), *got)
                free[i % 2] = pool.do(lambda e, dst=dst, buf=buf: e.tensor_tensor(
                    dst[1][:], buf, f32(dst[0][:]), ALU.subtract), e)
                e_mid_w.append(free[i % 2])

        once_done = [e_cols_t, e_bias, *e_mid_w, *e_blank_rows, *((s.sem, s.count) for s in (dve, pool, act))]

        class Router:

            def __init__(self, stack, name, depth, slots, passed, turn_bank, small_bank):
                self.slots, self.passed, self.depth = slots, passed, depth
                self.turn_bank, self.small_bank = turn_bank, small_bank
                self.rows = [tile(stack, f"{name}_rows{i}", [P, ROW]) for i in range(depth)]
                self.feat = [tile(stack, f"{name}_feat{i}", [P, KD, P]) for i in range(2 * GROUP)]
                self.stat = [tile(stack, f"{name}_stat{i}", [P, 10]) for i in range(2 * GROUP)]
                self.result = [tile(stack, f"{name}_pass{i}", [P, D]) for i in range(4)]
                self.log = tile(stack, f"{name}_log", [P, GROUP, E])
                self.tmp = tile(stack, f"{name}_tmp", [P, GROUP, E])
                self.hot = tile(stack, f"{name}_hot", [P, GROUP, E])
                self.hot_bf = tile(stack, f"{name}_hotb", [P, GROUP, E], BF16)
                self.ex = tile(stack, f"{name}_ex", [P, GROUP, E])
                self.small = tile(stack, f"{name}_small", [P, 8, GROUP])
                self.dest = [tile(stack, f"{name}_dest{i}", [P, GROUP], I32) for i in range(2)]
                self.sent, self.stored = {}, {}
                self.filled, self.std, self.norm, self.featd = {}, {}, {}, {}
                self.row_free = {}
                self.pass_free = {}
                self.group_done = self.bank_read = None
                self.group_logits = {}
                self.recent = tile(stack, f"{name}_seen", [P, E])

            def row(self, n):
                return self.rows[n % self.depth]

            def place_free(self, n):
                return self.row_free.get(n - self.depth, ())

            def stats(self, n, ready):
                st = self.stat[n % (2 * GROUP)]
                x = self.row(n)[:, D:2 * D]
                e = dve.do(lambda e: e.bn_stats(st[:, 0:6], x), ready, self.norm.get(n - 2 * GROUP))
                e = dve.do(lambda e: e.bn_aggr(st[:, 6:8], st[:, 0:6]), e)
                e = dve.do(lambda e: e.tensor_scalar(st[:, 7:8], st[:, 7:8], EPS, None, ALU.add), e)
                self.std[n] = pool.do(lambda e: e.tensor_tensor(st[:, 8:9], st[:, 7:8], minus_half[:], ALU.pow), e)

            def normed(self, n, bank_free):
                st, row, feat = self.stat[n % (2 * GROUP)], self.row(n), self.feat[n % (2 * GROUP)]
                self.norm[n] = dve.do(lambda e: e.tensor_scalar(
                    row[:, 0:D], row[:, D:2 * D], st[:, 6:7], st[:, 8:9], ALU.subtract, ALU.mult),
                    self.std[n], *self.place_free(n))
                dst = self.turn_bank
                for k in range(KD):
                    e = turn(dst[:, k * P:(k + 1) * P], row[:, k * P:(k + 1) * P], self.norm[n], *bank_free,
                             signal=k == KD - 1)
                self.featd[n] = act.do(lambda e: e.copy(feat[:], dst[:, 0:D].rearrange("p (k t) -> p k t", k=KD)),
                                       e, self.group_logits.get(n // GROUP - 2) if n >= 2 * GROUP else None)
                return self.featd[n]

            def logits(self, g, bank_free):
                dst = self.small_bank[:, 0:GROUP * E].rearrange("p (t e) -> p t e", t=GROUP)
                for i in range(GROUP):
                    n = g * GROUP + i
                    feat = self.feat[n % (2 * GROUP)]
                    for k in range(KD):
                        pe.quiet(lambda e, i=i, k=k, feat=feat: e.matmul(
                            dst[:, i], feat[:, k], switch_w[:, k], start=k == 0, stop=False,
                            skip_group_check=True), self.featd[n], *bank_free)
                    e = pe.do(lambda e, i=i: e.matmul(dst[:, i], ones_row[:], switch_b[:], start=False, stop=True,
                                                      skip_group_check=True))
                self.group_logits[g] = e

            def choose(self, g):
                src = self.small_bank[:, 0:GROUP * E].rearrange("p (t e) -> p t e", t=GROUP)
                sm, wide = self.small, [P, GROUP, E]
                e = dve.do(lambda e: e.tensor_copy(self.log[:], src), self.group_logits[g], self.group_done)
                self.bank_read = e
                e_max = dve.do(lambda e: e.tensor_reduce(sm[:, 0], self.log[:], AX, ALU.max), e)
                e = dve.do(lambda e: e.tensor_tensor(
                    self.tmp[:], self.log[:], sm[:, 0].unsqueeze(2).broadcast_to(wide), ALU.is_ge), e_max)
                e = dve.do(lambda e: e.tensor_tensor(self.tmp[:], self.tmp[:], first_wins, ALU.mult), e)
                e = dve.do(lambda e: e.tensor_reduce(sm[:, 1], self.tmp[:], AX, ALU.max), e)
                e = dve.do(lambda e: e.tensor_tensor(
                    self.hot[:], first_wins, sm[:, 1].unsqueeze(2).broadcast_to(wide), ALU.is_equal), e)
                self.hot_ready = dve.do(lambda e: e.tensor_copy(self.hot_bf[:], self.hot[:]), e)
                self.shifted = dve.do(lambda e: e.tensor_tensor(
                    self.log[:], self.log[:], sm[:, 0].unsqueeze(2).broadcast_to(wide), ALU.subtract), e)

            def count(self, g):
                dst = self.small_bank[:, 0:GROUP * E].rearrange("p (t e) -> p t e", t=GROUP)
                self.exped = act.do(lambda e: e.activation(self.ex[:], self.log[:], ACT.Exp), self.shifted)
                e_seen = self.seen_ready
                for i in range(GROUP):
                    pe.quiet(lambda e, i=i: e.matmul(dst[:, i], upto[:], self.hot_bf[:, i], start=True, stop=False,
                                                     skip_group_check=True), self.hot_ready, self.bank_read)
                    for j in range(i):
                        pe.quiet(lambda e, i=i, j=j: e.matmul(dst[:, i], ones_bf[:], self.hot_bf[:, j], start=False,
                                                              stop=False, skip_group_check=True))
                    e = pe.do(lambda e, i=i, g=g: e.matmul(dst[:, i], ones_bf[:], seen_sum[:, g % 2], start=False,
                                                           stop=True, skip_group_check=True), e_seen)
                self.counted = e

            def dispatch(self, g):
                src = self.small_bank[:, 0:GROUP * E].rearrange("p (t e) -> p t e", t=GROUP)
                sm, dest = self.small, self.dest[g % 2]
                e = dve.do(lambda e: e.tensor_tensor(self.tmp[:], src, self.hot[:], ALU.mult), self.counted)
                self.bank_read = e
                e1 = dve.do(lambda e: e.tensor_reduce(sm[:, 2], self.tmp[:], AX, ALU.add), e)
                e = dve.do(lambda e: e.tensor_tensor(self.tmp[:], slot_base, self.hot[:], ALU.mult), e1)
                e2 = dve.do(lambda e: e.tensor_reduce(sm[:, 3], self.tmp[:], AX, ALU.add), e)
                e = dve.do(lambda e: e.tensor_scalar(sm[:, 4], sm[:, 2], float(CAP), float(NOWHERE), ALU.is_gt,
                                                     ALU.mult), e1)
                e = dve.do(lambda e: e.scalar_tensor_tensor(out=sm[:, 3], in0=sm[:, 2], scalar=-1.0, in1=sm[:, 3],
                                                            op0=ALU.add, op1=ALU.add), e2)
                e_dest = dve.do(lambda e: e.tensor_tensor(dest[:], sm[:, 3], sm[:, 4], ALU.add), e,
                                *[self.sent.get(n) for n in range((g - 2) * GROUP, (g - 1) * GROUP)])
                if g + 1 < NG:
                    e = dve.do(lambda e: e.tensor_reduce(
                        self.recent[:], self.hot[:].rearrange("p t e -> p e t"), AX, ALU.add), e_dest)
                    self.seen_ready = dve.do(lambda e, g=g: e.tensor_tensor(
                        seen_sum[:, (g + 1) % 2], self.recent[:], seen_sum[:, g % 2], ALU.add), e)
                e = dve.do(lambda e: e.tensor_reduce(sm[:, 5], self.ex[:], AX, ALU.add), self.exped)
                e = dve.do(lambda e: e.reciprocal(sm[:, 6], sm[:, 5]), e)
                e = dve.do(lambda e: e.reciprocal(sm[:, 7], sm[:, 6]), e)
                e_scale = dve.do(lambda e: e.scalar_tensor_tensor(
                    out=sm[:, 5], in0=sm[:, 6], scalar=0.5, in1=sm[:, 7], op0=ALU.mult, op1=ALU.mult), e)
                for i in range(GROUP):
                    n = g * GROUP + i
                    row, res = self.row(n), self.result[n % 4]
                    ea = dve.do(lambda e, i=i, row=row: e.tensor_copy(row[:, SC_COL:SC_COL + 1], sm[:, 5, i:i + 1]),
                                e_scale)
                    eb = dve.do(lambda e, n=n, row=row: e.tensor_copy(
                        row[:, ID_COL:ID_COL + 1].bitcast(I32), token_id[:, n:n + 1]), *self.place_free(n))
                    self.sent[n] = pool.dma(r_scatter, lambda e, i=i, row=row, dest=dest: e.indirect_dma_start(
                        self.slots, bass.IndirectOffsetOnAxis(ap=dest[:, i:i + 1], axis=0), row[:], None,
                        bounds_check=SLOTS - 1, oob_is_err=False), ea, eb, e_dest, self.norm[n], *e_blank_rows)
                    ec = dve.do(lambda e, i=i, row=row, res=res: e.scalar_tensor_tensor(
                        out=res[:], in0=row[:, 0:D], scalar=sm[:, 5, i:i + 1], in1=row[:, D:2 * D], op0=ALU.mult,
                        op1=ALU.add), e_scale, self.stored.get(n - 4))
                    self.stored[n] = sp.dma(r_store, lambda e, n=n, res=res: e.dma_start(
                        self.passed[n * P:(n + 1) * P, :], res[:]), ec)
                    self.row_free[n] = (self.sent[n], ec)
                self.group_done = ec

        class Experts:

            def __init__(self, bufs):
                self.raw1, self.raw2, self.w1s, self.w2s = bufs

            def allocate(self, stack, name):
                self.slot_rows = [tile(stack, f"{name}_slots{i}", [P, ST, ROW]) for i in range(3)]
                self.xt = tile(stack, f"{name}_xt", [P, KD, CAP])
                self.xts = [[tile(stack, f"{name}_xt{b}{i}", [P, KD, CAP], F32R) for i in range(2)] for b in range(2)]
                self.h = [tile(stack, f"{name}_h{i}", [P, 2, CAP]) for i in range(2)]
                self.hs = [[tile(stack, f"{name}_h{b}{i}", [P, 2, CAP], F32R) for i in range(2)] for b in range(4)]
                self.fin = [tile(stack, f"{name}_fin{i}", [P, D]) for i in range(4)]
                self.b2_raw = tile(stack, f"{name}_b2raw", [1, E * D])
                self.b2_low = tile(stack, f"{name}_b2low", [1, E * D], F32R)
                self.b2_rows = tile(stack, f"{name}_b2rows", [2, E * D], F32R)

            def load_weights(self, e_, *after):
                r1, r2 = self.raw1, self.raw2
                a = sp.dma(r_weight, lambda e: e.dma_start(r1[:], w1[e_].rearrange("(k p) n -> p k n", p=P)), *after)
                b = sp.dma(r_weight, lambda e: e.dma_start(r2[:], w2[e_].rearrange("(k p) n -> p k n", p=P)), *after)
                return a, b

            def split_weights(self, e_, got, *after):
                (h1, l1), (h2, l2) = self.w1s[e_ % 2], self.w2s[e_ % 2]
                r1, r2 = self.raw1, self.raw2
                e = dve.do(lambda e: e.tensor_copy(h1[:], r1[:]), got[0], *after)
                a = dve.do(lambda e: e.tensor_tensor(l1[:], r1[:], f32(h1[:]), ALU.subtract), e)
                e = act.do(lambda e: e.copy(h2[:], r2[:]), got[1], *after)
                b = pool.do(lambda e: e.tensor_tensor(l2[:], r2[:], f32(h2[:]), ALU.subtract), e)
                return a, b

            def run(self, slots, target, first_split, arrived, passed):
                split = {0: first_split}
                got_rows, xt_ready = {}, {}
                proj_done, fin_sent = {}, {}
                e = sp.dma(r_const, lambda e: e.dma_start(self.b2_raw[:], b2.rearrange("e d -> (e d)").unsqueeze(0)),
                           *arrived)
                e = dve.do(lambda e: e.tensor_copy(self.b2_rows[0:1, :], self.b2_raw[:]), e, *arrived)
                e = dve.do(lambda e: e.tensor_tensor(self.b2_low[:], self.b2_raw[:], f32(self.b2_rows[0:1, :]),
                                                     ALU.subtract), e)
                e_b2 = sp.dma(r_const, lambda e: e.dma_start(f32(self.b2_rows[1:2, :]), f32(self.b2_low[:])), e)

                def load_rows(x):
                    buf = self.slot_rows[x % 3]
                    got_rows[x] = sp.dma(r_rows, lambda e: e.dma_start(
                        buf[:], slots[x * CAP:(x + 1) * CAP, :].rearrange("(s p) r -> p s r", p=P)),
                        *arrived, *fin_read.get(x - 3, ()))

                fin_read = {}

                def turn_rows(x):
                    buf = self.slot_rows[x % 3]
                    dst = bank[4]
                    for k in range(KD):
                        for s in range(ST):
                            e = turn(dst[:, k * CAP + s * P:k * CAP + (s + 1) * P], buf[:, s, k * P:(k + 1) * P],
                                     got_rows[x], xt_ready.get(x - 1), signal=(k, s) == (KD - 1, ST - 1))
                    src = dst[:].rearrange("p (k c) -> p k c", k=KD)
                    hi, lo = self.xts[x % 2]
                    a = act.do(lambda e: e.copy(self.xt[:], src), e, xt_lo.get(x - 1))
                    b = act.do(lambda e: e.copy(hi[:], src), e, up_done.get(x - 2))
                    xt_lo[x] = dve.do(lambda e: e.tensor_tensor(lo[:], self.xt[:], f32(hi[:]), ALU.subtract), a, b)
                    xt_ready[x] = b

                xt_lo, up_done, h_ready = {}, {}, {}
                pairs = KE // 2

                def up(x, j):
                    u = x * pairs + j
                    dst = bank[u % 2]
                    hi, lo = self.w1s[x % 2]
                    xh, xl = self.xts[x % 2]
                    for i in range(2):
                        m = 2 * j + i
                        for k in range(KD):
                            e = product(dst[:, i * CAP:(i + 1) * CAP],
                                        (hi[:, k, m * P:(m + 1) * P], lo[:, k, m * P:(m + 1) * P]),
                                        (xh[:, k], xl[:, k]), k == 0, k == KD - 1,
                                        xt_lo[x], *split[x], h_read.get(u - 2), signal=k == KD - 1)
                    up_done[x] = e
                    h32 = self.h[u % 2]
                    hh, hl = self.hs[u % 4]
                    for i in range(2):
                        m = 2 * j + i
                        a = act.do(lambda e, i=i, m=m: e.activation(
                            h32[:, i], dst[:, i * CAP:(i + 1) * CAP], ACT.Relu,
                            bias=cols[:, x * KE + m:x * KE + m + 1]), e, h_lo.get(u - 2))
                    h_read[u] = a
                    b = dve.do(lambda e: e.tensor_copy(hh[:], h32[:]), a, down_done.get(u - 4))
                    h_lo[u] = dve.do(lambda e: e.tensor_tensor(hl[:], h32[:], f32(hh[:]), ALU.subtract), b)

                h_read, h_lo, down_done = {}, {}, {}

                def down(x, j):
                    u = x * pairs + j
                    dst = bank[2 + x % 2]
                    hi, lo = self.w2s[x % 2]
                    hh, hl = self.hs[u % 4]
                    if j == 0:
                        for s in range(ST):
                            add_bias(dst[:, s * D:(s + 1) * D], self.b2_rows[:, x * D:(x + 1) * D], s == 0, e_b2,
                                     *fin_read.get(x - 2, ()))
                    for i in range(2):
                        m = 2 * j + i
                        for s in range(ST):
                            e = product(dst[:, s * D:(s + 1) * D],
                                        (hh[:, i, s * P:(s + 1) * P], hl[:, i, s * P:(s + 1) * P]),
                                        (hi[:, m], lo[:, m]), False, m == KE - 1, h_lo[u],
                                        signal=(i, s) == (1, ST - 1))
                    down_done[u] = e
                    if j == pairs - 1:
                        finish(x, e)

                def finish(x, e_y):
                    dst, buf = bank[2 + x % 2], self.slot_rows[x % 3]
                    reads = []
                    for s in range(ST):
                        f = self.fin[(x * ST + s) % 4]
                        e = dve.do(lambda e, s=s, f=f: e.scalar_tensor_tensor(
                            out=f[:], in0=dst[:, s * D:(s + 1) * D], scalar=buf[:, s, SC_COL:SC_COL + 1],
                            in1=buf[:, s, D:2 * D], op0=ALU.mult, op1=ALU.add), e_y, fin_sent.get(x * ST + s - 4))
                        fin_sent[x * ST + s] = pool.dma(r_scatter, lambda e, s=s, f=f: e.indirect_dma_start(
                            target, bass.IndirectOffsetOnAxis(ap=buf[:, s, ID_COL:ID_COL + 1].bitcast(I32), axis=0),
                            f[:], None, bounds_check=T - 1, oob_is_err=False), e, *passed)
                        reads += [e, fin_sent[x * ST + s]]
                    fin_read[x] = reads

                lag = 2
                load_rows(0)
                turn_rows(0)
                load_rows(1)
                load_rows(2)
                for u in range(E * pairs + lag):
                    x, j = divmod(u, pairs)
                    if x < E:
                        if j == 0 and x + 1 < E:
                            got = self.load_weights(x + 1, *split[x])
                        up(x, j)
                        if j == 2 and x + 1 < E:
                            turn_rows(x + 1)
                    if u >= lag:
                        px, pj = divmod(u - lag, pairs)
                        down(px, pj)
                        if pj == pairs - 1:
                            if px + 3 < E:
                                load_rows(px + 3)
                    if x < E and j == lag - 1 and x + 1 < E:
                        split[x + 1] = self.split_weights(x + 1, got, down_done.get((x - 1) * pairs + pairs - 1),
                                                          up_done.get(x - 1))
                return [v for v in fin_sent.values()] + [(s.sem, s.count) for s in (pe, dve, act)]

        def weight_buffers(stack, name):
            return (tile(stack, f"{name}_raw1", [P, KD, EH]), tile(stack, f"{name}_raw2", [P, KE, D]),
                    [[tile(stack, f"{name}_w1{b}{i}", [P, KD, EH], F32R) for i in range(2)] for b in range(2)],
                    [[tile(stack, f"{name}_w2{b}{i}", [P, KE, D], F32R) for i in range(2)] for b in range(2)])

        def everything():
            return [(s.sem, s.count) for s in (pe, dve, act, pool)] + [v for r in rings for v in r.all()]

        with ExitStack() as phase:
            ex_a = Experts(weight_buffers(phase, "a"))
            with ExitStack() as routing:
                for s in (dve, act, pool, sp, pe):
                    s.wait(*once_done)
                ra = Router(routing, "ra", 8, slots_dram[0], mid_rows, bank[5], bank[6])
                ra.seen_ready = e_consts
                dve.wait(e_mh, e_ids, e_consts)
                pool.wait(e_mh)
                pe.wait(e_sw, e_sb, e_upto, e_ones, e_consts)
                loaded = {}

                def load_x(n):
                    row = ra.row(n)
                    loaded[n] = sp.dma(r_x, lambda e: e.dma_start(row[:, D:2 * D], x_rows[n * P:(n + 1) * P, :]),
                                       *ra.place_free(n))

                for n in range(2 * GROUP):
                    load_x(n)
                got0 = ex_a.load_weights(0)
                ready = None
                for g in range(NG):
                    tiles = range(g * GROUP, (g + 1) * GROUP)
                    for n in tiles:
                        ra.stats(n, loaded[n])
                    if g == 0:
                        split0 = ex_a.split_weights(0, got0)
                    for n in tiles:
                        ready = ra.normed(n, (ready,))
                    ra.logits(g, (ra.bank_read,))
                    ra.choose(g)
                    ra.count(g)
                    ra.dispatch(g)
                    for n in tiles:
                        if n + 2 * GROUP < NT:
                            load_x(n + 2 * GROUP)
                arrived = everything()
            for s in (dve, act, pool, sp, pe):
                s.wait(*arrived)
            with ExitStack() as work:
                ex_a.allocate(work, "xa")
                ex_a.run(slots_dram[0], mid_rows, split0, arrived, arrived)
                done_a = everything()

        for s in (dve, act, pool, sp, pe):
            s.wait(*done_a)
        with ExitStack() as mid:
            rb = Router(mid, "rb", 8, slots_dram[1], out_rows, bank[0], bank[4])
            e_zero = dve.do(lambda e: e.memset(seen_sum[:, 0], 0.0))
            rb.seen_ready = e_zero

            def many(name, n, shape, dt=F32):
                return [tile(mid, f"{name}{i}", shape, dt) for i in range(n)]

            x1 = many("x1_", 9, [P, D])
            z = many("z_", 6, [P, D])
            zn = many("zn_", 2, [P, D])
            stz = many("stz_", 3, [P, 10])
            stn = many("stn_", 3, [P, 10])
            sth = many("sth_", 3, [P, 10])
            xnt = many("xnt_", 1, [P, KD, P])
            xnts = [many(f"xnts{i}_", 2, [P, KD, P], F32R) for i in range(2)]
            soft = many("soft_", 1, [P, 2 * D])
            feats = many("feats_", 2, [P, 2 * D])
            vals = many("vals_", 3, [P, D])
            prod_ = many("prod_", 6, [P, 4, D])
            stt = many("stt_", 1, [P, D])
            score = many("score_", 2, [P, D])
            ssum = many("ssum_", 2, [P, 2, HEADS])
            ot = many("ot_", 1, [P, D])
            ots = [many(f"ots{i}_", 2, [P, D], F32R) for i in range(2)]
            xa = many("xa_", 3, [P, D])
            xr = many("xr_", 12, [P, D])
            hn = many("hn_", 2, [P, D])
            hnt = many("hnt_", 1, [P, KD, P])
            hnts = [many(f"hnts{i}_", 2, [P, KD, GT], F32R) for i in range(2)]
            hid = many("hid_", 2, [P, GT])
            hids = [many(f"hids{i}_", 3, [P, GT], F32R) for i in range(2)]
            B_TURN, B_QK, B_V, B_ACC, B_S, B_UP, B_DOWN = 0, 1, 2, 3, 4, 5, 6

            ev = {}

            def got(*key):
                return ev.get(key)

            last_read = {i: None for i in range(8)}

            def rstd(st, e, key):
                e = dve.do(lambda e: e.bn_aggr(st[:, 6:8], st[:, 0:6]), e)
                e = dve.do(lambda e: e.tensor_scalar(st[:, 7:8], st[:, 7:8], EPS, None, ALU.add), e)
                ev[key] = pool.do(lambda e: e.tensor_tensor(st[:, 8:9], st[:, 7:8], minus_half[:], ALU.pow), e)

            def load(n):
                ev["x1", n] = sp.dma(r_x, lambda e: e.dma_start(x1[n % 9][:], mid_rows[n * P:(n + 1) * P, :]),
                                     got("xr", n - 9), got("z", n - 9))

            def stat_x(n):
                st = stz[n % 3]
                e = dve.do(lambda e: e.bn_stats(st[:, 0:6], x1[n % 9][:]), got("x1", n), got("z", n - 3))
                rstd(st, e, ("stz", n))

            def norm_z(n):
                st, s2 = stz[n % 3], stn[n % 3]
                e = ev["z", n] = dve.do(lambda e: e.tensor_scalar(
                    z[n % 6][:], x1[n % 9][:], st[:, 6:7], st[:, 8:9], ALU.subtract, ALU.mult),
                    got("stz", n), got("xa", n - 6))
                e = dve.do(lambda e: e.bn_stats(s2[:, 0:6], z[n % 6][:]), e, got("zn", n - 3))
                rstd(s2, e, ("stn", n))

            def norm_zn(n):
                st = stn[n % 3]
                ev["zn", n] = dve.do(lambda e: e.tensor_scalar(
                    zn[n % 2][:], z[n % 6][:], st[:, 6:7], st[:, 8:9], ALU.subtract, ALU.mult),
                    got("stn", n), got("znT", n - 2))

            def turn_zn(n):
                dst = bank[B_TURN]
                for k in range(KD):
                    e = turn(dst[:, k * P:(k + 1) * P], zn[n % 2][:, k * P:(k + 1) * P], ev["zn", n],
                             last_read[B_TURN], signal=k == KD - 1)
                ev["znT", n] = e
                for k in range(KD):
                    w, b = cols[:, C_LN + k:C_LN + k + 1], cols[:, C_LN + KD + k:C_LN + KD + k + 1]
                    a = act.do(lambda e, k=k, w=w, b=b: e.activation(
                        xnt[0][:, k], dst[:, k * P:(k + 1) * P], ACT.Identity, bias=b, scale=w),
                        e, got("xnl", n - 1))
                    a = act.do(lambda e, k=k, w=w, b=b: e.activation(
                        xnts[0][n % 2][:, k], dst[:, k * P:(k + 1) * P], ACT.Identity, bias=b, scale=w),
                        got("qkv", n - 2))
                ev["xnh", n] = last_read[B_TURN] = a

            def low_zn(n):
                ev["xnl", n] = dve.do(lambda e: e.tensor_tensor(
                    xnts[1][n % 2][:], xnt[0][:], f32(xnts[0][n % 2][:]), ALU.subtract), ev["xnh", n],
                    got("qkv", n - 2))

            def qkv(n):
                hi, lo = xnts[0][n % 2], xnts[1][n % 2]
                for b, c0, w in ((B_QK, 0, 2 * D), (B_V, 2 * D, D)):
                    dst = bank[b][:, 0:w]
                    add_bias(dst, bias_rows[:, c0:c0 + w], True, last_read[b], ev["xnl", n], ev["xnh", n])
                    for k in range(KD):
                        e = product(dst, (hi[:, k], lo[:, k]),
                                    (qkv_w[0][:, k, c0:c0 + w], qkv_w[1][:, k, c0:c0 + w]), False, k == KD - 1,
                                    signal=k == KD - 1)
                    ev["qkv", n] = e
                    if b == B_QK:
                        e_qk = e
                a = act.do(lambda e: e.activation(soft[0][:], bank[B_QK][:], ACT.Relu, scale=-1.0), e_qk,
                           got("feat", n - 1))
                ev["soft", n] = act.do(lambda e: e.activation(soft[0][:], soft[0][:], ACT.Exp, scale=-1.0), a)
                ev["v", n] = last_read[B_V] = act.do(lambda e: e.copy(vals[n % 3][:], bank[B_V][:, 0:D]), e,
                                                     got("pv", n - 3), got("pvp", n - 3))

            def feat(n):
                ev["feat", n] = last_read[B_QK] = dve.do(lambda e: e.scalar_tensor_tensor(
                    out=feats[n % 2][:], in0=bank[B_QK][:], scalar=0.0, in1=soft[0][:], op0=ALU.max, op1=ALU.add),
                    ev["soft", n], got("pk", n - 2), got("pkp", n - 2))

            slot_of = [0]
            place_free = {}

            def products(n, kind):
                chunks = []
                for c in range(4):
                    i = slot_of[0] % 6
                    slot_of[0] += 1
                    dst = prod_[i][:].rearrange("p j (a b) -> p j a b", a=HEADS)
                    wide = [P, 4, HEADS, HEADS]
                    if kind == "k":
                        f = feats[n % 2]
                        left = f[:, 0:D].rearrange("p (h d) -> p d h", d=HD)[:, 4 * c:4 * c + 4]
                        right = f[:, D:2 * D].rearrange("p (h d) -> p d h", d=HD)[:, 4 * c:4 * c + 4]
                        left = left.unsqueeze(3).broadcast_to(wide)
                        right = right.unsqueeze(2).broadcast_to(wide)
                        need = ev["feat", n]
                    else:
                        left = score[n % 2][:].rearrange("p (h g) -> p g h", g=HEADS)[:, 4 * c:4 * c + 4]
                        right = vals[n % 3][:].rearrange("p (g e) -> p g e", e=HD)[:, 4 * c:4 * c + 4]
                        left = left.unsqueeze(3).broadcast_to(wide)
                        right = right.unsqueeze(2).broadcast_to(wide)
                        need = ev["score", n]
                    eng = pool if c == 3 else dve
                    e = eng.do(lambda e, dst=dst, left=left, right=right: e.tensor_tensor(dst, left, right, ALU.mult),
                               need, ev["v", n], place_free.get(i))
                    ev["p" + kind + ("p" if c == 3 else ""), n] = e
                    chunks.append((i, e))
                ev["chunks" + kind, n] = chunks

            def gather_products(n, kind):
                dst = bank[B_ACC]
                chunks = ev["chunks" + kind, n]
                for c, (i, e) in enumerate(chunks):
                    for j in range(4):
                        for half in range(KD):
                            first, last = c == 0 and j == 0, c == 3 and j == 3
                            done = turn(dst[:, half * P:(half + 1) * P], prod_[i][:, j, half * P:(half + 1) * P], e,
                                        last_read[B_ACC], start=first and half == 0, stop=last,
                                        signal=j == 3 and half == KD - 1)
                    place_free[i] = done
                return done

            def scores_t(n):
                e = gather_products(n, "k")
                ev["stt", n] = last_read[B_ACC] = act.do(lambda e: e.copy(stt[0][:], bank[B_ACC][:, 0:D]), e,
                                                         got("sback", n - 1))

            def scores_back(n):
                dst = bank[B_S]
                for k in range(KD):
                    e = turn(dst[:, k * P:(k + 1) * P], stt[0][:, k * P:(k + 1) * P], ev["stt", n], last_read[B_S],
                             signal=k == KD - 1)
                ev["sback", n] = e

            def scale_scores(n):
                s = bank[B_S][:, 0:D].rearrange("p (h g) -> p h g", g=HEADS)
                sm = ssum[n % 2]
                e = dve.do(lambda e: e.tensor_reduce(sm[:, 0], s, AX, ALU.add), ev["sback", n])
                e = dve.do(lambda e: e.tensor_scalar(sm[:, 0], sm[:, 0], ATTN_EPS, None, ALU.add), e)
                e = dve.do(lambda e: e.reciprocal(sm[:, 1], sm[:, 0]), e)
                ev["score", n] = last_read[B_S] = dve.do(lambda e: e.tensor_tensor(
                    score[n % 2][:].rearrange("p (h g) -> p h g", g=HEADS), s,
                    sm[:, 1].unsqueeze(2).broadcast_to([P, HEADS, HEADS]), ALU.mult), e,
                    got("pv", n - 2), got("pvp", n - 2))

            def attended(n):
                e = gather_products(n, "v")
                a = act.do(lambda e: e.copy(ot[0][:], bank[B_ACC][:, 0:D]), e, got("otl", n - 1))
                ev["oth", n] = last_read[B_ACC] = act.do(lambda e: e.copy(ots[0][n % 2][:], bank[B_ACC][:, 0:D]),
                                                         got("wo", n - 2))

            def low_o(n):
                ev["otl", n] = dve.do(lambda e: e.tensor_tensor(
                    ots[1][n % 2][:], ot[0][:], f32(ots[0][n % 2][:]), ALU.subtract), ev["oth", n], got("wo", n - 2))

            def project(n):
                dst = bank[B_V][:, 0:D]
                add_bias(dst, bias_rows[:, BO:BO + D], True, last_read[B_V], ev["otl", n])
                for k in range(KD):
                    e = product(dst, (ots[0][n % 2][:, k * P:(k + 1) * P], ots[1][n % 2][:, k * P:(k + 1) * P]),
                                (o_w[0][:, k], o_w[1][:, k]), False, k == KD - 1, signal=k == KD - 1)
                ev["wo", n] = e

            def residual(n):
                st = sth[n % 3]
                e = ev["xa", n] = last_read[B_V] = dve.do(lambda e: e.tensor_tensor(
                    xa[n % 3][:], bank[B_V][:, 0:D], z[n % 6][:], ALU.add), ev["wo", n], got("xr", n - 3),
                    got("hn", n - 3))
                ev["xr", n] = pool.do(lambda e: e.tensor_tensor(xr[n % 12][:], x1[n % 9][:], xa[n % 3][:], ALU.add), e,
                                      got("x2", n - 12))
                e = dve.do(lambda e: e.bn_stats(st[:, 0:6], xa[n % 3][:]), e, got("hn", n - 3))
                rstd(st, e, ("sth", n))

            def norm_h(n):
                st = sth[n % 3]
                ev["hn", n] = dve.do(lambda e: e.tensor_scalar(
                    hn[n % 2][:], xa[n % 3][:], st[:, 6:7], st[:, 8:9], ALU.subtract, ALU.mult), ev["sth", n],
                    got("hnT", n - 2))

            def turn_h(n):
                g, t = divmod(n, GROUP)
                dst = bank[B_TURN]
                for k in range(KD):
                    e = turn(dst[:, k * P:(k + 1) * P], hn[n % 2][:, k * P:(k + 1) * P], ev["hn", n],
                             last_read[B_TURN], signal=k == KD - 1)
                ev["hnT", n] = e
                for k in range(KD):
                    w, b = (cols[:, C_LN + i * KD + k:C_LN + i * KD + k + 1] for i in (2, 3))
                    a = act.do(lambda e, k=k, w=w, b=b: e.activation(
                        hnt[0][:, k], dst[:, k * P:(k + 1) * P], ACT.Identity, bias=b, scale=w), e, got("hnl", n - 1))
                    a = act.do(lambda e, k=k, w=w, b=b: e.activation(
                        hnts[0][g % 2][:, k, t * P:(t + 1) * P], dst[:, k * P:(k + 1) * P], ACT.Identity, bias=b,
                        scale=w), got("up", g - 2, KM - 1))
                ev["hnh", n] = last_read[B_TURN] = a

            def low_h(n):
                g, t = divmod(n, GROUP)
                ev["hnl", n] = dve.do(lambda e: e.tensor_tensor(
                    hnts[1][g % 2][:, :, t * P:(t + 1) * P], hnt[0][:], f32(hnts[0][g % 2][:, :, t * P:(t + 1) * P]),
                    ALU.subtract), ev["hnh", n], got("up", g - 2, KM - 1))

            def up_mid(g, m):
                dst, u = bank[B_UP], g * KM + m
                for k in range(KD):
                    e = product(dst[:], (up_w[0][:, k, m * P:(m + 1) * P], up_w[1][:, k, m * P:(m + 1) * P]),
                                (hnts[0][g % 2][:, k], hnts[1][g % 2][:, k]), k == 0, k == KD - 1,
                                ev["hnl", g * GROUP + GROUP - 1], last_read[B_UP], signal=k == KD - 1)
                ev["up", g, m] = e
                bias = cols[:, C_FCB + m:C_FCB + m + 1]
                a = act.do(lambda e: e.activation(hid[u % 2][:], dst[:], ACT.Gelu, bias=bias), e, got("hl", u - 2))
                a = act.do(lambda e: e.activation(hids[0][u % 3][:], dst[:], ACT.Gelu, bias=bias), got("down", u - 3))
                ev["hh", u] = last_read[B_UP] = a
                ev["hl", u] = pool.do(lambda e: e.tensor_tensor(
                    hids[1][u % 3][:], hid[u % 2][:], f32(hids[0][u % 3][:]), ALU.subtract), a, got("down", u - 3))

            def down_mid(g, m):
                u = g * KM + m
                for t in range(GROUP):
                    dst = bank[B_DOWN + t // 2][:, (t % 2) * D:(t % 2 + 1) * D]
                    if m == 0:
                        add_bias(dst, bias_rows[:, PB:PB + D], t % 2 == 0, last_read[B_DOWN + t // 2])
                    e = product(dst, (hids[0][u % 3][:, t * P:(t + 1) * P], hids[1][u % 3][:, t * P:(t + 1) * P]),
                                (down_w[0][:, m], down_w[1][:, m]), False, m == KM - 1, ev["hl", u], ev["hh", u],
                                signal=t == GROUP - 1)
                ev["down", u] = e

            def x2(g):
                for t in range(GROUP):
                    n = g * GROUP + t
                    src = bank[B_DOWN + t // 2][:, (t % 2) * D:(t % 2 + 1) * D]
                    ev["x2", n] = last_read[B_DOWN + t // 2] = dve.do(lambda e, n=n, src=src: e.tensor_tensor(
                        rb.row(n)[:, D:2 * D], src, xr[n % 12][:], ALU.add), ev["down", g * KM + KM - 1],
                        ev["xr", n], *rb.place_free(n))

            def when(first, n, step):
                return n >= first and (n - first) % step == 0 and (n - first) // step < (NT if step == 1 else NG)

            for n in range(3):
                load(n)
            for s in range(NT + 24):
                def on(k, f):
                    if 0 <= s - k < NT:
                        f(s - k)

                on(-3, load)
                on(2, norm_zn)
                on(6, norm_h)
                on(2, turn_zn)
                on(5, project)
                on(6, turn_h)
                on(3, lambda n: products(n, "k"))
                on(2, low_zn)
                on(6, low_h)
                on(5, residual)
                on(3, scores_t)
                on(2, qkv)
                on(4, lambda n: products(n, "v"))
                g, j = divmod(s - 10, GROUP)
                fc = 0 <= g < NG
                if fc:
                    up_mid(g, 2 * j)
                on(3, scores_back)
                on(2, feat)
                on(3, scale_scores)
                gp, jp = divmod(s - 11, GROUP)
                if 0 <= gp < NG:
                    down_mid(gp, 2 * jp + 1)
                if when(14, s, GROUP):
                    x2((s - 14) // GROUP)
                    for n in range(s - 14, s - 14 + GROUP):
                        rb.stats(n, ev["x2", n])
                on(4, attended)
                on(1, norm_z)
                on(0, stat_x)
                if fc:
                    up_mid(g, 2 * j + 1)
                    down_mid(g, 2 * j)
                on(4, low_o)
                for first in (15, 16):
                    if when(first, s, GROUP):
                        n0 = s - first + 2 * (first - 15)
                        for n in (n0, n0 + 1):
                            last_read[B_TURN] = rb.normed(n, (last_read[B_TURN],))
                if when(17, s, GROUP):
                    rb.logits((s - 17) // GROUP, (last_read[B_S],))
                    rb.choose((s - 17) // GROUP)
                    last_read[B_S] = rb.bank_read
                if when(18, s, GROUP):
                    rb.bank_read = last_read[B_S]
                    rb.count((s - 18) // GROUP)
                    rb.dispatch((s - 18) // GROUP)
                    last_read[B_S] = rb.bank_read
            done_mid = everything()

        for s in (dve, act, pool, sp, pe):
            s.wait(*done_mid)
        with ExitStack() as phase:
            ex_b = Experts(weight_buffers(phase, "b"))
            ex_b.allocate(phase, "xb")
            got0 = ex_b.load_weights(0)
            ex_b.run(slots_dram[1], out_rows, ex_b.split_weights(0, got0), done_mid, done_mid)

        sp.wait(*[v for r in rings for v in r.all()])

        block = ctx.enter_context(nc.Block())

        @block.sync
        def _(eng):
            sp.play(eng)

        @block.gpsimd
        def _(eng):
            pool.play(eng)

        @block.scalar
        def _(eng):
            act.play(eng)

        @block.vector
        def _(eng):
            dve.play(eng)

        @block.tensor
        def _(eng):
            pe.play(eng)


_INS = ["L0_attn_q_x", "L0_attn_ln1_w", "L0_attn_ln1_b", "L0_attn_wq", "L0_attn_bq", "L0_attn_wk", "L0_attn_bk",
        "L0_attn_wv", "L0_attn_bv", "L0_attn_wo", "L0_attn_bo", "L0_attn_ln2_w", "L0_attn_ln2_b", "L0_attn_fc_w",
        "L0_attn_fc_b", "L0_attn_proj_w", "L0_attn_proj_b", "L0_ffn_w_switch", "L0_ffn_b_switch", "L0_ffn_w1",
        "L0_ffn_b1", "L0_ffn_w2", "L0_ffn_b2"]
_OUTS = [((8, 512, 256), "float32")]


def kernel(**inputs):
    import numpy as _np
    import concourse.bacc as _bacc
    from concourse import mybir as _mybir
    from concourse.bass_utils import run_bass_kernel_spmd as _run

    nc = _bacc.Bacc("TRN2", target_bir_lowering=False, num_devices=1)
    arrays, args = {}, []
    for name in _INS:
        a = _np.ascontiguousarray(inputs[name])
        arrays[f"in_{name}_dram"] = a
        args.append(nc.dram_tensor(f"in_{name}_dram", a.shape, _mybir.dt.from_np(a.dtype), kind="ExternalInput").ap())
    for i, (shape, dtype) in enumerate(_OUTS):
        dt = _mybir.dt.from_np(_np.dtype(dtype))
        args.append(nc.dram_tensor(f"out_{i}_dram", shape, dt, kind="ExternalOutput").ap())
    build(nc, *args)
    r = _run(nc, [arrays], core_ids=[0])
    return r.results[0]["out_0_dram"]
```

```python
from contextlib import ExitStack

import concourse.bass as bass
from concourse import mybir

F32 = mybir.dt.float32
F32R = mybir.dt.float32r
BF16 = mybir.dt.bfloat16
I32 = mybir.dt.int32
ALU = mybir.AluOpType
ACT = mybir.ActivationFunctionType
AX = mybir.AxisListType.X

P = 128
GROUP = 4
EPS = 1e-5
ATTN_EPS = 1e-6
CAP_FACTOR = 0.5


class Stream:

    def __init__(self, sem):
        self.sem, self.count, self.queue, self.seen = sem, 0, [], {}

    def _waits(self, after):
        need = {}
        for event in after:
            if event is not None:
                sem, value = event
                if self.seen.get(id(sem), 0) < value:
                    self.seen[id(sem)] = value
                    need[id(sem)] = (sem, value)
        for sem, value in need.values():
            self.queue.append(lambda eng, sem=sem, value=value: eng.wait_ge(sem, value))

    def do(self, instruction, *after):
        self._waits(after)
        self.count += 1
        self.queue.append(lambda eng: instruction(eng).then_inc(self.sem, 1))
        return self.sem, self.count

    def quiet(self, instruction, *after):
        self._waits(after)
        self.queue.append(instruction)

    def dma(self, ring, transfer, *after):
        sem, value, before = ring.next()
        self._waits((*after, before))
        self.queue.append(lambda eng: transfer(eng).then_inc(sem, 16))
        return sem, value

    def wait(self, *after):
        self._waits(after)

    def play(self, eng):
        for step in self.queue:
            step(eng)


class Ring:

    def __init__(self, sems):
        self.sems, self.values, self.used = sems, [0] * len(sems), 0

    def next(self):
        i = self.used % len(self.sems)
        before = (self.sems[i], self.values[i]) if self.values[i] else None
        self.values[i] += 16
        self.used += 1
        return self.sems[i], self.values[i], before

    def all(self):
        return [(s, v) for s, v in zip(self.sems, self.values) if v]


def build(nc, x_in, ln1_w, ln1_b, wq, bq, wk, bk, wv, bv, wo, bo, ln2_w, ln2_b,
          fc_w, fc_b, proj_w, proj_b, w_switch, b_switch, w1, b1, w2, b2, out):
    B, N, D = x_in.shape
    T = B * N
    NT = T // P
    NG = NT // GROUP
    KD = D // P
    HEADS = 16
    HD = D // HEADS
    HID = fc_w.shape[1]
    KM = HID // P
    E = b_switch.shape[0]
    CAP = int(CAP_FACTOR * T / E)
    SLOTS = E * CAP
    ST = CAP // P
    EH = w1.shape[2]
    KE = EH // P
    GT = GROUP * P
    NOWHERE = 1 << 16
    assert KD == 2 and HEADS * HD == D and KE % 2 == 0 and ST == 2

    x_rows = x_in.rearrange("b n d -> (b n) d")
    out_rows = out.rearrange("b n d -> (b n) d")
    tables = [nc.dram_tensor(f"table{i}", [SLOTS, 2], F32).ap() for i in range(2)]
    mid_rows = nc.dram_tensor("mid_rows", [T, D], F32).ap()
    late_rows = nc.dram_tensor("late_rows", [T, D], F32).ap()

    with ExitStack() as ctx:
        def sem(name):
            return ctx.enter_context(nc.semaphore(name))

        def ring(name, n):
            return Ring([sem(f"{name}{i}") for i in range(n)])

        pe, dve, act, pool, sp = (Stream(sem(f"s_{n}")) for n in ("pe", "dve", "act", "pool", "sp"))
        rings = []

        def new_ring(name, n):
            rings.append(ring(name, n))
            return rings[-1]

        r_const = new_ring("d_const", 8)
        r_weight = new_ring("d_weight", 4)
        r_x = new_ring("d_x", 8)
        r_rows = new_ring("d_rows", 2)
        r_gather = new_ring("d_gather", 8)
        r_store = new_ring("d_store", 8)
        r_scatter = new_ring("d_scatter", 12)
        r_final = new_ring("d_final", 4)

        def tile(stack, name, shape, dt=F32):
            return stack.enter_context(nc.sbuf_tensor(name, shape, dt))

        bank = [ctx.enter_context(nc.psum_tensor(f"bank{i}", [P, 512], F32)) for i in range(8)]

        ident = tile(ctx, "ident", [P, P])
        upto = tile(ctx, "upto", [P, P], BF16)
        ones_bf = tile(ctx, "ones_bf", [P, P], BF16)
        ones_row = tile(ctx, "ones_row", [1, P])
        ones_two = tile(ctx, "ones_two", [2, P], F32R)
        token_id = tile(ctx, "token_id", [P, NT], I32)
        expert_i = tile(ctx, "expert_i", [P, GROUP, E], I32)
        first_wins = tile(ctx, "first_wins", [P, GROUP, E])
        switch_w = tile(ctx, "switch_w", [P, KD, E])
        switch_b = tile(ctx, "switch_b", [1, E])
        col_rows = E * KE + KM + 4 * KD
        cols = tile(ctx, "cols", [P, col_rows])
        C_FCB = E * KE
        C_LN = C_FCB + KM
        BO, PB = 3 * D, 4 * D
        bias_rows = tile(ctx, "bias_rows", [2, 5 * D], F32R)
        b2_rows = tile(ctx, "b2_rows", [2, E * D], F32R)
        seen_sum = tile(ctx, "seen_sum", [P, 2, E], BF16)
        minus_half = tile(ctx, "minus_half", [P, GROUP])
        e_mh = pool.do(lambda e: e.memset(minus_half[:], -0.5))

        BIAS = 2 * D
        with ExitStack() as once:
            col_src = tile(once, "col_src", [col_rows, P])
            bias_raw = tile(once, "bias_raw", [2, (5 + E) * D])
            bias_high = [tile(once, f"bias_high{i}", [2, BIAS], F32R) for i in range(2)]
            low_row = tile(once, "low_row", [2, 1])
            blank = tile(once, "blank", [P, SLOTS // P, 2])

        qkv_w = [tile(ctx, f"qkv_w{i}", [P, KD, 3 * D], F32R) for i in range(2)]
        o_w = [tile(ctx, f"o_w{i}", [P, KD, D], F32R) for i in range(2)]
        up_w = [tile(ctx, f"up_w{i}", [P, KD, HID], F32R) for i in range(2)]
        down_w = [tile(ctx, f"down_w{i}", [P, KM, D], F32R) for i in range(2)]

        def f32(ap):
            return ap.bitcast(F32)

        def product(dst, left, right, first, last, *after, signal=True):
            (lh, ll), (rh, rl) = left, right
            pe.quiet(lambda e: e.matmul(dst, lh, rh, start=first, stop=False, skip_group_check=True), *after)
            pe.quiet(lambda e: e.matmul(dst, lh, rl, start=False, stop=False, skip_group_check=True))
            go = pe.do if signal else pe.quiet
            return go(lambda e: e.matmul(dst, ll, rh, start=False, stop=last, skip_group_check=True))

        def add_bias(dst, rows, first, *after):
            pe.quiet(lambda e: e.matmul(dst, ones_two[:, 0:P], rows, start=first, stop=False,
                                        skip_group_check=True), *after)

        def turn(dst, src, *after, start=True, stop=True, signal=True):
            go = pe.do if signal else pe.quiet
            return go(lambda e: e.matmul(dst, src, ident[:], is_transpose=True, start=start, stop=stop,
                                         skip_group_check=True), *after)

        e_ident0 = pool.do(lambda e: e.memset(ident[:], 0.0))
        e_upto0 = pool.do(lambda e: e.memset(upto[:], 1.0))
        e_blank0 = pool.do(lambda e: e.memset(blank[:], 0.0))
        e_ident = pool.do(lambda e: e.affine_select(
            out=ident[:], in_=ident[:], compare_op=ALU.not_equal, fill=1.0, base=0,
            pattern=[[-1, P]], channel_multiplier=1), e_ident0)
        e_upto = pool.do(lambda e: e.affine_select(
            out=upto[:], in_=upto[:], compare_op=ALU.is_ge, fill=0.0, base=0,
            pattern=[[1, P]], channel_multiplier=-1), e_upto0)
        e_blank = pool.do(lambda e: e.memset(blank[:, :, 0].bitcast(I32), NOWHERE), e_blank0)
        e_ids = pool.do(lambda e: e.iota(token_id[:], pattern=[[P, NT]], base=0, channel_multiplier=1))
        e_iota = pool.do(lambda e: e.iota(expert_i[:], pattern=[[0, GROUP], [-1, E]], base=E, channel_multiplier=0))
        e_ones = dve.do(lambda e: e.memset(ones_bf[:], 1.0))
        dve.do(lambda e: e.memset(ones_row[:], 1.0))
        dve.do(lambda e: e.memset(f32(ones_two[:]), 1.0))
        dve.do(lambda e: e.memset(seen_sum[:], 0.0))
        e = dve.do(lambda e: e.memset(low_row[:], -1.0))
        e_low_row = dve.do(lambda e: e.memset(low_row[0:1, :], 0.0), e)
        e_consts = dve.do(lambda e: e.tensor_copy(first_wins[:], expert_i[:]), e_iota)

        def load_constants():
            nonlocal e_sw, e_sb
            e_sw = sp.dma(r_const, lambda e: e.dma_start(switch_w[:], w_switch.rearrange("(k p) e -> p k e", p=P)))
            e_sb = sp.dma(r_const, lambda e: e.dma_start(switch_b[:], b_switch.unsqueeze(0)))
            col_parts = [(b1.rearrange("e (m p) -> (e m) p", p=P), E * KE), (fc_b.rearrange("(m p) -> m p", p=P), KM)]
            col_parts += [(v.rearrange("(m p) -> m p", p=P), KD) for v in (ln1_w, ln1_b, ln2_w, ln2_b)]
            at = 0
            for src, n in col_parts:
                e_cols.append(sp.dma(r_const, lambda e, src=src, at=at, n=n: e.dma_start(col_src[at:at + n, :], src)))
                at += n
            parts = [(v.unsqueeze(0), i * D, D) for i, v in enumerate((bq, bk, bv, bo, proj_b))]
            parts.append((b2.rearrange("e d -> (e d)").unsqueeze(0), 5 * D, E * D))
            for v, c, n in parts:
                e_brow.append(sp.dma(r_const, lambda e, v=v, c=c, n=n: e.dma_start(
                    bias_raw[:, c:c + n], v.broadcast_to([2, n]))))

        def use_constants():
            e = pe.do(lambda e: e.matmul(bank[0][:, 0:col_rows], col_src[:], ident[0:col_rows, 0:col_rows],
                                         is_transpose=True, start=True, stop=True), e_ident, *e_cols)
            last = dve.do(lambda e: e.tensor_copy(cols[:], bank[0][:, 0:col_rows]), e)
            done = [None, None]
            for u, c in enumerate(range(0, (5 + E) * D, BIAS)):
                n = min(BIAS, (5 + E) * D - c)
                high = bias_high[u % 2][:, 0:n]
                pieces = [(bias_rows, c, c, min(c + n, 5 * D)), (b2_rows, max(c, 5 * D) - 5 * D, max(c, 5 * D), c + n)]
                e = dve.do(lambda e, c=c, n=n, high=high: e.tensor_copy(high, bias_raw[:, c:c + n]), *e_brow,
                           done[u % 2])
                for dst, d0, a, b in pieces:
                    if a < b:
                        done[u % 2] = dve.do(lambda e, dst=dst, d0=d0, a=a, b=b, c=c, high=high:
                                             e.scalar_tensor_tensor(
                                                 out=dst[:, d0:d0 + b - a], in0=f32(high[:, a - c:b - c]),
                                                 scalar=low_row[:, 0:1], in1=bias_raw[:, a:b], op0=ALU.mult,
                                                 op1=ALU.add), e, e_low_row)
            return [last, *done]

        e_sw = e_sb = None
        e_cols, e_brow, e_blank_rows = [], [], []

        def blank_table(i):
            e_blank_rows.append(sp.dma(r_store, lambda e: e.dma_start(
                tables[i].rearrange("(p c) r -> p c r", p=P), blank[:]), e_blank))

        class Router:

            def __init__(self, stack, name, depth, unit_depth, table, passed):
                self.table, self.passed, self.depth, self.unit_depth = table, passed, depth, unit_depth
                self.plain = [tile(stack, f"{name}_plain{i}", [P, D]) for i in range(depth)]
                self.unit = [tile(stack, f"{name}_unit{i}", [P, D]) for i in range(self.unit_depth)]
                self.feat = [tile(stack, f"{name}_feat{i}", [P, KD, P]) for i in range(2 * GROUP)]
                self.stat = [tile(stack, f"{name}_stat{i}", [P, GROUP, 6]) for i in range(2)]
                self.mean_var = [tile(stack, f"{name}_mv{i}", [P, GROUP, 2]) for i in range(2)]
                self.rstd = [tile(stack, f"{name}_rstd{i}", [P, GROUP]) for i in range(2)]
                self.result = [tile(stack, f"{name}_pass{i}", [P, D]) for i in range(GROUP)]
                self.tmp = tile(stack, f"{name}_tmp", [P, GROUP, E])
                self.hot = [tile(stack, f"{name}_hot{i}", [P, GROUP, E], BF16) for i in range(2)]
                self.ex = [tile(stack, f"{name}_ex{i}", [P, GROUP, E]) for i in range(2)]
                self.recent = tile(stack, f"{name}_recent", [P, E])
                self.best = [tile(stack, f"{name}_best{i}", [P, 2, GROUP]) for i in range(2)]
                self.small = tile(stack, f"{name}_small", [P, 6, GROUP])
                self.entry = [tile(stack, f"{name}_entry{i}", [P, GROUP, 2]) for i in range(2)]
                self.dest = [tile(stack, f"{name}_dest{i}", [P, GROUP], I32) for i in range(2)]
                self.sent, self.stored, self.norm, self.featd, self.logits_done = {}, {}, {}, {}, {}
                self.hot_ready, self.exped, self.counted, self.chosen, self.dispatched = {}, {}, {}, {}, {}
                self.result_made = {}
                self.seen_ready = None

            def row(self, n):
                return self.plain[n % self.depth]

            def place_free(self, n):
                return self.result_made.get(n - self.depth)

            def tiles(self, g):
                return range(g * GROUP, (g + 1) * GROUP)

            def stats(self, g, ready):
                st, mv, rs = self.stat[g % 2], self.mean_var[g % 2], self.rstd[g % 2]
                es = [dve.do(lambda e, i=i, n=n: e.bn_stats(st[:, i], self.row(n)[:]), ready[n])
                      for i, n in enumerate(self.tiles(g))]
                es = [dve.do(lambda e, i=i: e.bn_aggr(mv[:, i], st[:, i]), es[i], self.norm.get((g - 1) * GROUP - 1))
                      for i in range(GROUP)]
                e = pool.do(lambda e: e.tensor_scalar(rs[:], mv[:, :, 1], EPS, None, ALU.add), *es,
                            self.norm.get((g - 1) * GROUP - 1))
                self.std = pool.do(lambda e: e.tensor_tensor(rs[:], rs[:], minus_half[:], ALU.pow), e)

            def normed(self, n, dst, *bank_free):
                g, i = divmod(n, GROUP)
                mv, rs, row, feat = self.mean_var[g % 2], self.rstd[g % 2], self.row(n), self.feat[n % (2 * GROUP)]
                unit = self.unit[n % self.unit_depth]
                self.norm[n] = dve.do(lambda e: e.tensor_scalar(
                    unit[:], row[:], mv[:, i, 0:1], rs[:, i:i + 1], ALU.subtract, ALU.mult),
                    self.std, self.result_made.get(n - self.unit_depth))
                for k in range(KD):
                    e = turn(dst[:, k * P:(k + 1) * P], unit[:, k * P:(k + 1) * P], self.norm[n], *bank_free,
                             signal=k == KD - 1)
                self.featd[n] = act.do(lambda e: e.copy(feat[:], dst[:, 0:D].rearrange("p (k t) -> p k t", k=KD)),
                                       e, self.logits_done.get(g - 2))
                return self.featd[n]

            def logits(self, g, dst, *bank_free):
                self.dst = dst = dst[:, 0:GROUP * E].rearrange("p (t e) -> p t e", t=GROUP)
                for i, n in enumerate(self.tiles(g)):
                    feat = self.feat[n % (2 * GROUP)]
                    for k in range(KD):
                        pe.quiet(lambda e, i=i, k=k, feat=feat: e.matmul(
                            dst[:, i], feat[:, k], switch_w[:, k], start=k == 0, stop=False,
                            skip_group_check=True), self.featd[n], *bank_free)
                    e = pe.do(lambda e, i=i: e.matmul(dst[:, i], ones_row[:], switch_b[:], start=False, stop=True,
                                                      skip_group_check=True))
                self.logits_done[g] = e

            def choose(self, g):
                src, best, wide = self.dst, self.best[g % 2], [P, GROUP, E]
                hot, ex = self.hot[g % 2], self.ex[g % 2]
                e_max = dve.do(lambda e: e.tensor_reduce(best[:, 0], src, AX, ALU.max), self.logits_done[g],
                               self.dispatched.get(g - 2))
                e = dve.do(lambda e: e.tensor_tensor(
                    self.tmp[:], src, best[:, 0].unsqueeze(2).broadcast_to(wide), ALU.is_ge), e_max,
                    self.dispatched.get(g - 1))
                e_sub = dve.do(lambda e: e.tensor_tensor(
                    ex[:], src, best[:, 0].unsqueeze(2).broadcast_to(wide), ALU.subtract), e_max)
                e = dve.do(lambda e: e.tensor_tensor(self.tmp[:], self.tmp[:], first_wins[:], ALU.mult), e)
                e = dve.do(lambda e: e.tensor_reduce(best[:, 1], self.tmp[:], AX, ALU.max), e)
                self.hot_ready[g] = self.chosen[g] = dve.do(lambda e: e.tensor_tensor(
                    hot[:], first_wins[:], best[:, 1].unsqueeze(2).broadcast_to(wide), ALU.is_equal), e)
                self.shifted = e_sub
                return e_sub

            def soften(self, g):
                ex = self.ex[g % 2]
                self.exped[g] = act.do(lambda e: e.activation(ex[:], ex[:], ACT.Exp), self.shifted)

            def count(self, g, dst, *bank_free):
                self.cdst = dst = dst[:, 0:GROUP * E].rearrange("p (t e) -> p t e", t=GROUP)
                hot = self.hot[g % 2]
                for i in range(GROUP):
                    pe.quiet(lambda e, i=i: e.matmul(dst[:, i], upto[:], hot[:, i], start=True, stop=False,
                                                     skip_group_check=True), self.hot_ready[g], *bank_free)
                    for j in range(i):
                        pe.quiet(lambda e, i=i, j=j: e.matmul(dst[:, i], ones_bf[:], hot[:, j], start=False,
                                                              stop=False, skip_group_check=True))
                    e = pe.do(lambda e, i=i: e.matmul(dst[:, i], ones_bf[:], seen_sum[:, g % 2], start=False,
                                                      stop=True, skip_group_check=True), self.seen_ready)
                self.counted[g] = e
                if g + 1 < NG:
                    e = dve.do(lambda e: e.tensor_reduce(
                        self.recent[:], hot[:].rearrange("p t e -> p e t"), AX, ALU.add), self.hot_ready[g],
                        self.seen_ready)
                    self.seen_ready = dve.do(lambda e: e.tensor_tensor(
                        seen_sum[:, (g + 1) % 2], self.recent[:], seen_sum[:, g % 2], ALU.add), e,
                        self.counted.get(g - 1))

            def dispatch(self, g):
                src, sm, dest, best = self.cdst, self.small, self.dest[g % 2], self.best[g % 2]
                hot, ex, entry = self.hot[g % 2], self.ex[g % 2], self.entry[g % 2]
                entries_free = [self.sent.get(n) for n in self.tiles(g - 2)]
                e_read = dve.do(lambda e: e.tensor_tensor(self.tmp[:], src, hot[:], ALU.mult), self.counted[g],
                                self.chosen[g])
                e_s = dve.do(lambda e: e.tensor_reduce(sm[:, 3], ex[:], AX, ALU.add), self.exped[g],
                             self.dispatched.get(g - 1))
                e1 = dve.do(lambda e: e.tensor_reduce(sm[:, 0], self.tmp[:], AX, ALU.add), e_read)
                e_s = dve.do(lambda e: e.reciprocal(sm[:, 4], sm[:, 3]), e_s)
                e2 = dve.do(lambda e: e.tensor_scalar(sm[:, 1], sm[:, 0], float(CAP), float(NOWHERE), ALU.is_gt,
                                                      ALU.mult), e1)
                e3 = dve.do(lambda e: e.scalar_tensor_tensor(out=sm[:, 2], in0=best[:, 1], scalar=float(-CAP),
                                                             in1=sm[:, 0], op0=ALU.mult, op1=ALU.add), e1)
                e_s = dve.do(lambda e: e.reciprocal(sm[:, 5], sm[:, 4]), e_s)
                e_dest = dve.do(lambda e: e.scalar_tensor_tensor(
                    out=dest[:], in0=sm[:, 2], scalar=float(CAP * E - 1), in1=sm[:, 1], op0=ALU.add, op1=ALU.add),
                    e2, e3, *entries_free)
                e_scale = dve.do(lambda e: e.scalar_tensor_tensor(
                    out=entry[:, :, 1], in0=sm[:, 4], scalar=0.5, in1=sm[:, 5], op0=ALU.mult, op1=ALU.mult), e_s,
                    *entries_free)
                e_id = act.do(lambda e: e.copy(entry[:, :, 0].bitcast(I32), token_id[:, g * GROUP:(g + 1) * GROUP]),
                              *entries_free)
                for i, n in enumerate(self.tiles(g)):
                    row, unit, res = self.row(n), self.unit[n % self.unit_depth], self.result[n % GROUP]
                    self.sent[n] = pool.dma(r_scatter, lambda e, i=i: e.indirect_dma_start(
                        self.table, bass.IndirectOffsetOnAxis(ap=dest[:, i:i + 1], axis=0), entry[:, i], None,
                        bounds_check=SLOTS - 1, oob_is_err=False), e_id, e_scale, e_dest, *e_blank_rows)
                    e = dve.do(lambda e, i=i, row=row, res=res, unit=unit: e.scalar_tensor_tensor(
                        out=res[:], in0=unit[:], scalar=entry[:, i, 1:2], in1=row[:], op0=ALU.mult,
                        op1=ALU.add), e_scale, self.stored.get(n - GROUP))
                    self.stored[n] = sp.dma(r_store, lambda e, n=n, res=res: e.dma_start(
                        self.passed[n * P:(n + 1) * P, :], res[:]), e)
                    self.result_made[n] = e
                self.dispatched[g] = e
                return e_read

        class Experts:

            def __init__(self, bufs):
                self.raw, self.w1s, self.w2s = bufs
                self.got, self.split, self.up_done, self.down_done = {}, {}, {}, {}

            def allocate(self, stack, name):
                self.table = tile(stack, f"{name}_table", [P, E * ST, 2])
                self.token = tile(stack, f"{name}_token", [P, E * ST], I32)
                self.rows = [tile(stack, f"{name}_rows{i}", [P, ST, D]) for i in range(3)]
                self.unit = [tile(stack, f"{name}_unit{i}", [P, ST, D]) for i in range(2)]
                self.stat = [tile(stack, f"{name}_stat{i}", [P, ST, 6]) for i in range(2)]
                self.mean_var = [tile(stack, f"{name}_mv{i}", [P, ST, 2]) for i in range(2)]
                self.rstd = [tile(stack, f"{name}_rstd{i}", [P, ST]) for i in range(2)]
                self.xt = tile(stack, f"{name}_xt", [P, KD, CAP])
                self.xts = [[tile(stack, f"{name}_xt{b}{i}", [P, KD, CAP], F32R) for i in range(2)] for b in range(2)]
                self.h = [tile(stack, f"{name}_h{i}", [P, 2, CAP]) for i in range(2)]
                self.hs = [[tile(stack, f"{name}_h{b}{i}", [P, 2, CAP], F32R) for i in range(2)] for b in range(4)]
                self.fin = [tile(stack, f"{name}_fin{i}", [P, D]) for i in range(4)]

            def load_weights(self, x, c):
                r1, r2 = self.raw
                free = self.split.get((x - 1, c), (None, None))
                a, b = c * 2 * P, (c + 1) * 2 * P
                self.got[x, c] = (
                    sp.dma(r_weight, lambda e: e.dma_start(
                        r1[:, :, a:b], w1[x, :, a:b].rearrange("(k p) n -> p k n", p=P)), free[0]),
                    sp.dma(r_weight, lambda e: e.dma_start(
                        r2[:, 2 * c:2 * c + 2], w2[x, a:b].rearrange("(k p) n -> p k n", p=P)), free[1]))

            def split_weights(self, x, c):
                r1, r2 = self.raw
                (h1, l1), (h2, l2) = self.w1s[x % 2], self.w2s[x % 2]
                cut1, cut2 = (slice(None), slice(None), slice(c * 2 * P, (c + 1) * 2 * P)), (slice(None), slice(2 * c, 2 * c + 2))
                got1, got2 = self.got[x, c]
                u = (x - 2) * KE // 2 + c
                e = dve.do(lambda e: e.tensor_copy(h1[cut1], r1[cut1]), got1, self.up_done.get(u))
                e1 = dve.do(lambda e: e.tensor_tensor(l1[cut1], r1[cut1], f32(h1[cut1]), ALU.subtract), e)
                e = act.do(lambda e: e.copy(h2[cut2], r2[cut2]), got2, self.down_done.get(u))
                e2 = pool.do(lambda e: e.tensor_tensor(l2[cut2], r2[cut2], f32(h2[cut2]), ALU.subtract), e)
                self.split[x, c] = (e1, e2)

            def run(self, slot_table, source, target, arrived, passed, between=None):
                split, up_done, down_done = self.split, self.up_done, self.down_done
                got_rows, normed, turned, xt_ready, fin_read = {}, {}, {}, {}, {}
                fin_sent = {}
                table, token = self.table, self.token
                e_table = sp.dma(r_rows, lambda e: e.dma_start(
                    table[:], slot_table.rearrange("(c p) r -> p c r", p=P)), *arrived)
                e_token = dve.do(lambda e: e.tensor_scalar(token[:], table[:, :, 0].bitcast(I32), T - 1, None,
                                                           ALU.min), e_table)

                def load_rows(x):
                    buf = self.rows[x % 3]
                    got_rows[x] = [pool.dma(r_gather, lambda e, s=s: e.indirect_dma_start(
                        buf[:, s], None, source,
                        bass.IndirectOffsetOnAxis(ap=token[:, x * ST + s:x * ST + s + 1], axis=0)),
                        e_token, *arrived, *fin_read.get(x - 3, ())) for s in range(ST)]

                def norm_rows(x):
                    buf, unit = self.rows[x % 3], self.unit[x % 2]
                    st, mv, rs = self.stat[x % 2], self.mean_var[x % 2], self.rstd[x % 2]
                    es = [dve.do(lambda e, s=s: e.bn_stats(st[:, s], buf[:, s]), got_rows[x][s]) for s in range(ST)]
                    es = [dve.do(lambda e, s=s: e.bn_aggr(mv[:, s], st[:, s]), es[s]) for s in range(ST)]
                    e = pool.do(lambda e: e.tensor_scalar(rs[:], mv[:, :, 1], EPS, None, ALU.add), *es,
                                *normed.get(x - 2, ()))
                    e = pool.do(lambda e: e.tensor_tensor(rs[:], rs[:], minus_half[:, 0:ST], ALU.pow), e)
                    normed[x] = [dve.do(lambda e, s=s: e.tensor_scalar(
                        unit[:, s], buf[:, s], mv[:, s, 0:1], rs[:, s:s + 1], ALU.subtract, ALU.mult),
                        es[s], e, turned.get(x - 2)) for s in range(ST)]

                def turn_rows(x):
                    unit = self.unit[x % 2]
                    dst = bank[4]
                    for k in range(KD):
                        for s in range(ST):
                            e = turn(dst[:, k * CAP + s * P:k * CAP + (s + 1) * P], unit[:, s, k * P:(k + 1) * P],
                                     normed[x][s], xt_ready.get(x - 1), signal=(k, s) == (KD - 1, ST - 1))
                    turned[x] = e
                    src = dst[:].rearrange("p (k c) -> p k c", k=KD)
                    hi, lo = self.xts[x % 2]
                    a = act.do(lambda e: e.copy(self.xt[:], src), e, xt_lo.get(x - 1))
                    b = act.do(lambda e: e.copy(hi[:], src), e, up_done.get((x - 1) * pairs - 1))
                    xt_lo[x] = dve.do(lambda e: e.tensor_tensor(lo[:], self.xt[:], f32(hi[:]), ALU.subtract), a, b)
                    xt_ready[x] = b

                xt_lo = {}
                pairs = KE // 2

                def up(x, j):
                    u = x * pairs + j
                    dst = bank[u % 2]
                    hi, lo = self.w1s[x % 2]
                    xh, xl = self.xts[x % 2]
                    for i in range(2):
                        m = 2 * j + i
                        for k in range(KD):
                            e = product(dst[:, i * CAP:(i + 1) * CAP],
                                        (hi[:, k, m * P:(m + 1) * P], lo[:, k, m * P:(m + 1) * P]),
                                        (xh[:, k], xl[:, k]), k == 0, k == KD - 1,
                                        xt_lo[x], split[x, j][0], h_read.get(u - 2), signal=k == KD - 1)
                    up_done[u] = e
                    h32 = self.h[u % 2]
                    hh, hl = self.hs[u % 4]
                    for i in range(2):
                        m = 2 * j + i
                        a = act.do(lambda e, i=i, m=m: e.activation(
                            h32[:, i], dst[:, i * CAP:(i + 1) * CAP], ACT.Relu,
                            bias=cols[:, x * KE + m:x * KE + m + 1]), e, h_lo.get(u - 2))
                        a = act.do(lambda e, i=i, m=m: e.activation(
                            hh[:, i], dst[:, i * CAP:(i + 1) * CAP], ACT.Relu,
                            bias=cols[:, x * KE + m:x * KE + m + 1]), down_done.get(u - 4))
                    h_read[u] = a
                    h_lo[u] = dve.do(lambda e: e.tensor_tensor(hl[:], h32[:], f32(hh[:]), ALU.subtract), a)

                h_read, h_lo = {}, {}

                def down(x, j):
                    u = x * pairs + j
                    dst = bank[2 + x % 2]
                    hi, lo = self.w2s[x % 2]
                    hh, hl = self.hs[u % 4]
                    if j == 0:
                        for s in range(ST):
                            add_bias(dst[:, s * D:(s + 1) * D], b2_rows[:, x * D:(x + 1) * D], s == 0,
                                     *fin_read.get(x - 2, ()))
                    for i in range(2):
                        m = 2 * j + i
                        for s in range(ST):
                            e = product(dst[:, s * D:(s + 1) * D],
                                        (hh[:, i, s * P:(s + 1) * P], hl[:, i, s * P:(s + 1) * P]),
                                        (hi[:, m], lo[:, m]), False, m == KE - 1, h_lo[u], split[x, j][1],
                                        signal=(i, s) == (1, ST - 1))
                    down_done[u] = e
                    if j == pairs - 1:
                        finish(x, e)

                def finish(x, e_y):
                    dst, buf = bank[2 + x % 2], self.rows[x % 3]
                    reads = []
                    for s in range(ST):
                        f, c = self.fin[(x * ST + s) % 4], x * ST + s
                        e = dve.do(lambda e, s=s, f=f, c=c: e.scalar_tensor_tensor(
                            out=f[:], in0=dst[:, s * D:(s + 1) * D], scalar=table[:, c, 1:2],
                            in1=buf[:, s], op0=ALU.mult, op1=ALU.add), e_y, fin_sent.get(c - 4))
                        fin_sent[c] = pool.dma(r_scatter, lambda e, s=s, f=f, c=c: e.indirect_dma_start(
                            target, bass.IndirectOffsetOnAxis(ap=table[:, c, 0:1].bitcast(I32), axis=0),
                            f[:], None, bounds_check=T - 1, oob_is_err=False), e, *passed)
                        reads.append(e)
                    fin_read[x] = reads

                lag = 2
                for x in range(3):
                    load_rows(x)
                norm_rows(0)
                turn_rows(0)
                for u in range(E * pairs + lag):
                    x, j = divmod(u, pairs)
                    if x < E:
                        up(x, j)
                        if j == 1 and x + 1 < E:
                            norm_rows(x + 1)
                        if j == 2 and x + 1 < E:
                            turn_rows(x + 1)
                    if u >= lag:
                        px, pj = divmod(u - lag, pairs)
                        down(px, pj)
                        if pj == pairs - 1 and px + 3 < E:
                            load_rows(px + 3)
                    if x + 1 < E:
                        self.split_weights(x + 1, j)
                    if x + 2 < E:
                        self.load_weights(x + 2, j)
                    if x < E and between:
                        between(u)
                return [v for v in fin_sent.values()] + [(s.sem, s.count) for s in (pe, dve, act)]

        def weight_buffers(stack, name):
            raw = [tile(stack, f"{name}_raw{w}", [P, *shape]) for w, shape in enumerate(((KD, EH), (KE, D)))]
            even, odd = ([[tile(stack, f"{name}_w{b}{w}{i}", [P, *shape], F32R) for i in range(2)]
                          for w, shape in enumerate(((KD, EH), (KE, D)))] for b in range(2))
            return raw, [even[0], odd[0]], [even[1], odd[1]]

        def so_far(streams=(pe, dve, act, pool)):
            return [(s.sem, s.count) for s in streams]

        def everything():
            return so_far() + [v for r in rings for v in r.all()]

        with ExitStack() as phase:
            ex_a = Experts(weight_buffers(phase, "a"))
            ex_a.allocate(phase, "xa")
            piece_raw = [tile(phase, f"piece_raw{i}", [P, KM * D]) for i in range(2)]
        with ExitStack() as phase:
            for w, shape in enumerate(((KD, EH), (KE, D))):
                tile(phase, f"below_raw{w}", [P, *shape])
                tile(phase, f"below_high{w}", [P, *shape])
                tile(phase, f"below_low{w}", [P, *shape])
            ra = Router(phase, "ra", 6 * GROUP, 3 * GROUP, tables[0], mid_rows)
        ra.seen_ready = e_consts
        loaded = {}

        def load_x(n):
            row = ra.row(n)
            loaded[n] = sp.dma(r_x, lambda e: e.dma_start(row[:], x_rows[n * P:(n + 1) * P, :]),
                               ra.place_free(n))

        ra_bufs_free = []
        for n in range(GROUP):
            load_x(n)
        load_constants()
        for n in range(GROUP, 5 * GROUP):
            load_x(n)
        blank_table(0)
        for x in range(2):
            for c in range(KE // 2):
                if x == 0:
                    ex_a.load_weights(x, c)
        bank_free = [None] * 8
        for g in range(NG + 3):
            if 2 <= g < NG + 2:
                ra.logits(g - 2, bank[6], bank_free[6])
            if g < NG:
                ra.stats(g, loaded)
            if g == 0:
                constants_used = use_constants()
                pe.wait(e_upto, e_ones, e_consts, e_mh)
                act.wait(e_ids)
                pe.wait(e_sw, e_sb)
                bank_free[0] = constants_used[0]
            if g >= 3:
                bank_free[7] = ra.dispatch(g - 3)
                for n in ra.tiles(g + 2):
                    if n < NT:
                        load_x(n)
            if 1 <= g <= NG:
                for n in ra.tiles(g - 1):
                    bank_free[n % 4] = ra.normed(n, bank[n % 4], bank_free[n % 4])
            if 2 <= g < NG + 2:
                bank_free[6] = ra.choose(g - 2)
                ra.soften(g - 2)
                ra.count(g - 2, bank[7], bank_free[7])
            if 2 <= g < 2 + KE // 2:
                ex_a.split_weights(0, g - 2)
                ex_a.load_weights(1, g - 2)
        blank_table(1)
        arrived = everything()

        for s in (dve, act, pool, pe, sp):
            s.wait(*arrived)
        pieces = [
            (qkv_w, KD, [(wq, 0, D), (wk, D, D), (wv, 2 * D, D)]),
            (o_w, KD, [(wo, 0, D)]),
            (up_w, KD, [(fc_w, 0, HID)]),
            (down_w, KM, [(proj_w, 0, D)]),
        ]

        chunks = [(i, k, c) for i, (_, n, parts) in enumerate(pieces) for k in range(n)
                  for c in range(0, parts[-1][1] + parts[-1][2], D)]
        piece_got, piece_read = {}, {}

        def piece_view(i):
            _, n, parts = pieces[i]
            return piece_raw[i % 2][:, 0:n * (parts[-1][1] + parts[-1][2])].rearrange("p (k n) -> p k n", k=n)

        def load_piece(i):
            view = piece_view(i)
            piece_got[i] = [sp.dma(r_weight, lambda e, w=w, c=c, n=n: e.dma_start(
                view[:, :, c:c + n], w.rearrange("(k p) n -> p k n", p=P)), piece_read.get(i - 2))
                for w, c, n in pieces[i][2]]

        def middle_weights(u):
            if u == 0:
                load_piece(0)
                load_piece(1)
            elif u <= len(chunks):
                i, k, c = chunks[u - 1]
                view, (high, low) = piece_view(i), pieces[i][0]
                e = act.do(lambda e: e.copy(high[:, k, c:c + D], view[:, k, c:c + D]), *piece_got[i])
                piece_read[i] = dve.do(lambda e: e.tensor_tensor(
                    low[:, k, c:c + D], view[:, k, c:c + D], f32(high[:, k, c:c + D]), ALU.subtract), e)
                if i + 2 < len(pieces) and chunks[u][0] != i:
                    load_piece(i + 2)

        ex_a.run(tables[0], x_rows, mid_rows, arrived, arrived, middle_weights)
        done_a = everything()

        for s in (dve, act, pool, sp, pe):
            s.wait(*done_a)
        with ExitStack() as mid:
            rb = Router(mid, "rb", 2 * GROUP, 2 * GROUP, tables[1], out_rows)
            rb.seen_ready = dve.do(lambda e: e.memset(seen_sum[:, 0], 0.0))

            def many(name, n, shape, dt=F32):
                return [tile(mid, f"{name}{i}", shape, dt) for i in range(n)]

            x1 = many("x1_", 9, [P, D])
            z = many("z_", 6, [P, D])
            zn = many("zn_", 2, [P, D])
            stz = many("stz_", 3, [P, 10])
            stn = many("stn_", 3, [P, 10])
            sth = many("sth_", 3, [P, 10])
            xnt = many("xnt_", 1, [P, KD, P])
            xnts = [many(f"xnts{i}_", 2, [P, KD, P], F32R) for i in range(2)]
            soft = many("soft_", 1, [P, 2 * D])
            feats = many("feats_", 2, [P, 2 * D])
            vals = many("vals_", 3, [P, D])
            prod_ = many("prod_", 6, [P, 4, D])
            stt = many("stt_", 1, [P, D])
            score = many("score_", 2, [P, D])
            ssum = many("ssum_", 2, [P, 2, HEADS])
            ot = many("ot_", 1, [P, D])
            ots = [many(f"ots{i}_", 2, [P, D], F32R) for i in range(2)]
            xa = many("xa_", 3, [P, D])
            xr = many("xr_", 12, [P, D])
            hn = many("hn_", 2, [P, D])
            hnt = many("hnt_", 1, [P, KD, P])
            hnts = [many(f"hnts{i}_", 2, [P, KD, GT], F32R) for i in range(2)]
            hid = many("hid_", 2, [P, GT])
            hids = [many(f"hids{i}_", 3, [P, GT], F32R) for i in range(2)]
            B_TURN, B_QK, B_V, B_ACC, B_S, B_UP, B_DOWN = 0, 1, 2, 3, 4, 5, 6

            ev = {}

            def got(*key):
                return ev.get(key)

            last_read = {i: None for i in range(8)}

            def rstd(st, e, key):
                e = dve.do(lambda e: e.bn_aggr(st[:, 6:8], st[:, 0:6]), e)
                e = dve.do(lambda e: e.tensor_scalar(st[:, 7:8], st[:, 7:8], EPS, None, ALU.add), e)
                ev[key] = pool.do(lambda e: e.tensor_tensor(st[:, 8:9], st[:, 7:8], minus_half[:, 0:1], ALU.pow), e)

            def load(n):
                ev["x1", n] = sp.dma(r_x, lambda e: e.dma_start(x1[n % 9][:], mid_rows[n * P:(n + 1) * P, :]),
                                     got("xr", n - 9), got("z", n - 9))

            def stat_x(n):
                st = stz[n % 3]
                e = dve.do(lambda e: e.bn_stats(st[:, 0:6], x1[n % 9][:]), got("x1", n), got("z", n - 3))
                rstd(st, e, ("stz", n))

            def norm_z(n):
                st, s2 = stz[n % 3], stn[n % 3]
                e = ev["z", n] = dve.do(lambda e: e.tensor_scalar(
                    z[n % 6][:], x1[n % 9][:], st[:, 6:7], st[:, 8:9], ALU.subtract, ALU.mult),
                    got("stz", n), got("xa", n - 6))
                e = dve.do(lambda e: e.bn_stats(s2[:, 0:6], z[n % 6][:]), e, got("zn", n - 3))
                rstd(s2, e, ("stn", n))

            def norm_zn(n):
                st = stn[n % 3]
                ev["zn", n] = dve.do(lambda e: e.tensor_scalar(
                    zn[n % 2][:], z[n % 6][:], st[:, 6:7], st[:, 8:9], ALU.subtract, ALU.mult),
                    got("stn", n), got("znT", n - 2))

            def turn_zn(n):
                dst = bank[B_TURN]
                for k in range(KD):
                    e = turn(dst[:, k * P:(k + 1) * P], zn[n % 2][:, k * P:(k + 1) * P], ev["zn", n],
                             last_read[B_TURN], signal=k == KD - 1)
                ev["znT", n] = e
                for k in range(KD):
                    w, b = cols[:, C_LN + k:C_LN + k + 1], cols[:, C_LN + KD + k:C_LN + KD + k + 1]
                    a = act.do(lambda e, k=k, w=w, b=b: e.activation(
                        xnt[0][:, k], dst[:, k * P:(k + 1) * P], ACT.Identity, bias=b, scale=w),
                        e, got("xnl", n - 1))
                    a = act.do(lambda e, k=k, w=w, b=b: e.activation(
                        xnts[0][n % 2][:, k], dst[:, k * P:(k + 1) * P], ACT.Identity, bias=b, scale=w),
                        got("qkv", n - 2))
                ev["xnh", n] = last_read[B_TURN] = a

            def low_zn(n):
                ev["xnl", n] = dve.do(lambda e: e.tensor_tensor(
                    xnts[1][n % 2][:], xnt[0][:], f32(xnts[0][n % 2][:]), ALU.subtract), ev["xnh", n],
                    got("qkv", n - 2))

            def qkv(n):
                hi, lo = xnts[0][n % 2], xnts[1][n % 2]
                for b, c0, w in ((B_QK, 0, 2 * D), (B_V, 2 * D, D)):
                    dst = bank[b][:, 0:w]
                    add_bias(dst, bias_rows[:, c0:c0 + w], True, last_read[b], ev["xnl", n], ev["xnh", n])
                    for k in range(KD):
                        e = product(dst, (hi[:, k], lo[:, k]),
                                    (qkv_w[0][:, k, c0:c0 + w], qkv_w[1][:, k, c0:c0 + w]), False, k == KD - 1,
                                    signal=k == KD - 1)
                    ev["qkv", n] = e
                    if b == B_QK:
                        e_qk = e
                a = act.do(lambda e: e.activation(soft[0][:], bank[B_QK][:], ACT.Relu, scale=-1.0), e_qk,
                           got("feat", n - 1))
                ev["soft", n] = act.do(lambda e: e.activation(soft[0][:], soft[0][:], ACT.Exp, scale=-1.0), a)
                ev["v", n] = last_read[B_V] = act.do(lambda e: e.copy(vals[n % 3][:], bank[B_V][:, 0:D]), e,
                                                     got("pv", n - 3), got("pvp", n - 3))

            def feat(n):
                ev["feat", n] = last_read[B_QK] = dve.do(lambda e: e.scalar_tensor_tensor(
                    out=feats[n % 2][:], in0=bank[B_QK][:], scalar=0.0, in1=soft[0][:], op0=ALU.max, op1=ALU.add),
                    ev["soft", n], got("pk", n - 2), got("pkp", n - 2))

            slot_of = [0]
            place_free = {}

            def products(n, kind):
                chunks = []
                for c in range(4):
                    i = slot_of[0] % 6
                    slot_of[0] += 1
                    dst = prod_[i][:].rearrange("p j (a b) -> p j a b", a=HEADS)
                    wide = [P, 4, HEADS, HEADS]
                    if kind == "k":
                        f = feats[n % 2]
                        left = f[:, 0:D].rearrange("p (h d) -> p d h", d=HD)[:, 4 * c:4 * c + 4]
                        right = f[:, D:2 * D].rearrange("p (h d) -> p d h", d=HD)[:, 4 * c:4 * c + 4]
                        left = left.unsqueeze(3).broadcast_to(wide)
                        right = right.unsqueeze(2).broadcast_to(wide)
                        need = ev["feat", n]
                    else:
                        left = score[n % 2][:].rearrange("p (h g) -> p g h", g=HEADS)[:, 4 * c:4 * c + 4]
                        right = vals[n % 3][:].rearrange("p (g e) -> p g e", e=HD)[:, 4 * c:4 * c + 4]
                        left = left.unsqueeze(3).broadcast_to(wide)
                        right = right.unsqueeze(2).broadcast_to(wide)
                        need = ev["score", n]
                    eng = pool if c == 3 else dve
                    e = eng.do(lambda e, dst=dst, left=left, right=right: e.tensor_tensor(dst, left, right, ALU.mult),
                               need, ev["v", n], place_free.get(i))
                    ev["p" + kind + ("p" if c == 3 else ""), n] = e
                    chunks.append((i, e))
                ev["chunks" + kind, n] = chunks

            def gather_products(n, kind):
                dst = bank[B_ACC]
                chunks = ev["chunks" + kind, n]
                for c, (i, e) in enumerate(chunks):
                    for j in range(4):
                        for half in range(KD):
                            first, last = c == 0 and j == 0, c == 3 and j == 3
                            done = turn(dst[:, half * P:(half + 1) * P], prod_[i][:, j, half * P:(half + 1) * P], e,
                                        last_read[B_ACC], start=first and half == 0, stop=last,
                                        signal=j == 3 and half == KD - 1)
                    place_free[i] = done
                return done

            def scores_t(n):
                e = gather_products(n, "k")
                ev["stt", n] = last_read[B_ACC] = act.do(lambda e: e.copy(stt[0][:], bank[B_ACC][:, 0:D]), e,
                                                         got("sback", n - 1))

            def scores_back(n):
                dst = bank[B_S]
                for k in range(KD):
                    e = turn(dst[:, k * P:(k + 1) * P], stt[0][:, k * P:(k + 1) * P], ev["stt", n], last_read[B_S],
                             signal=k == KD - 1)
                ev["sback", n] = e

            def scale_scores(n):
                s = bank[B_S][:, 0:D].rearrange("p (h g) -> p h g", g=HEADS)
                sm = ssum[n % 2]
                e = dve.do(lambda e: e.tensor_reduce(sm[:, 0], s, AX, ALU.add), ev["sback", n])
                e = dve.do(lambda e: e.tensor_scalar(sm[:, 0], sm[:, 0], ATTN_EPS, None, ALU.add), e)
                e = dve.do(lambda e: e.reciprocal(sm[:, 1], sm[:, 0]), e)
                ev["score", n] = last_read[B_S] = dve.do(lambda e: e.tensor_tensor(
                    score[n % 2][:].rearrange("p (h g) -> p h g", g=HEADS), s,
                    sm[:, 1].unsqueeze(2).broadcast_to([P, HEADS, HEADS]), ALU.mult), e,
                    got("pv", n - 2), got("pvp", n - 2))

            def attended(n):
                e = gather_products(n, "v")
                a = act.do(lambda e: e.copy(ot[0][:], bank[B_ACC][:, 0:D]), e, got("otl", n - 1))
                ev["oth", n] = last_read[B_ACC] = act.do(lambda e: e.copy(ots[0][n % 2][:], bank[B_ACC][:, 0:D]),
                                                         got("wo", n - 2))

            def low_o(n):
                ev["otl", n] = dve.do(lambda e: e.tensor_tensor(
                    ots[1][n % 2][:], ot[0][:], f32(ots[0][n % 2][:]), ALU.subtract), ev["oth", n], got("wo", n - 2))

            def project(n):
                dst = bank[B_V][:, 0:D]
                add_bias(dst, bias_rows[:, BO:BO + D], True, last_read[B_V], ev["otl", n])
                for k in range(KD):
                    e = product(dst, (ots[0][n % 2][:, k * P:(k + 1) * P], ots[1][n % 2][:, k * P:(k + 1) * P]),
                                (o_w[0][:, k], o_w[1][:, k]), False, k == KD - 1, signal=k == KD - 1)
                ev["wo", n] = e

            def residual(n):
                st = sth[n % 3]
                e = ev["xa", n] = last_read[B_V] = dve.do(lambda e: e.tensor_tensor(
                    xa[n % 3][:], bank[B_V][:, 0:D], z[n % 6][:], ALU.add), ev["wo", n], got("xr", n - 3),
                    got("hn", n - 3))
                ev["xr", n] = pool.do(lambda e: e.tensor_tensor(xr[n % 12][:], x1[n % 9][:], xa[n % 3][:], ALU.add), e,
                                      got("x2", n - 12))
                e = dve.do(lambda e: e.bn_stats(st[:, 0:6], xa[n % 3][:]), e, got("hn", n - 3))
                rstd(st, e, ("sth", n))

            def norm_h(n):
                st = sth[n % 3]
                ev["hn", n] = dve.do(lambda e: e.tensor_scalar(
                    hn[n % 2][:], xa[n % 3][:], st[:, 6:7], st[:, 8:9], ALU.subtract, ALU.mult), ev["sth", n],
                    got("hnT", n - 2))

            def turn_h(n):
                g, t = divmod(n, GROUP)
                dst = bank[B_TURN]
                for k in range(KD):
                    e = turn(dst[:, k * P:(k + 1) * P], hn[n % 2][:, k * P:(k + 1) * P], ev["hn", n],
                             last_read[B_TURN], signal=k == KD - 1)
                ev["hnT", n] = e
                for k in range(KD):
                    w, b = (cols[:, C_LN + i * KD + k:C_LN + i * KD + k + 1] for i in (2, 3))
                    a = act.do(lambda e, k=k, w=w, b=b: e.activation(
                        hnt[0][:, k], dst[:, k * P:(k + 1) * P], ACT.Identity, bias=b, scale=w), e, got("hnl", n - 1))
                    a = act.do(lambda e, k=k, w=w, b=b: e.activation(
                        hnts[0][g % 2][:, k, t * P:(t + 1) * P], dst[:, k * P:(k + 1) * P], ACT.Identity, bias=b,
                        scale=w), got("up", g - 2, KM - 1))
                ev["hnh", n] = last_read[B_TURN] = a

            def low_h(n):
                g, t = divmod(n, GROUP)
                ev["hnl", n] = dve.do(lambda e: e.tensor_tensor(
                    hnts[1][g % 2][:, :, t * P:(t + 1) * P], hnt[0][:], f32(hnts[0][g % 2][:, :, t * P:(t + 1) * P]),
                    ALU.subtract), ev["hnh", n], got("up", g - 2, KM - 1))

            def up_mid(g, m):
                dst, u = bank[B_UP], g * KM + m
                for k in range(KD):
                    e = product(dst[:], (up_w[0][:, k, m * P:(m + 1) * P], up_w[1][:, k, m * P:(m + 1) * P]),
                                (hnts[0][g % 2][:, k], hnts[1][g % 2][:, k]), k == 0, k == KD - 1,
                                ev["hnl", g * GROUP + GROUP - 1], last_read[B_UP], signal=k == KD - 1)
                ev["up", g, m] = e
                bias = cols[:, C_FCB + m:C_FCB + m + 1]
                a = act.do(lambda e: e.activation(hid[u % 2][:], dst[:], ACT.Gelu, bias=bias), e, got("hl", u - 2))
                a = act.do(lambda e: e.activation(hids[0][u % 3][:], dst[:], ACT.Gelu, bias=bias), got("down", u - 3))
                ev["hh", u] = last_read[B_UP] = a
                ev["hl", u] = pool.do(lambda e: e.tensor_tensor(
                    hids[1][u % 3][:], hid[u % 2][:], f32(hids[0][u % 3][:]), ALU.subtract), a, got("down", u - 3))

            def down_mid(g, m):
                u = g * KM + m
                for t in range(GROUP):
                    dst = bank[B_DOWN + t // 2][:, (t % 2) * D:(t % 2 + 1) * D]
                    if m == 0:
                        add_bias(dst, bias_rows[:, PB:PB + D], t % 2 == 0, last_read[B_DOWN + t // 2])
                    e = product(dst, (hids[0][u % 3][:, t * P:(t + 1) * P], hids[1][u % 3][:, t * P:(t + 1) * P]),
                                (down_w[0][:, m], down_w[1][:, m]), False, m == KM - 1, ev["hl", u], ev["hh", u],
                                signal=t == GROUP - 1)
                ev["down", u] = e

            def x2(g):
                for t in range(GROUP):
                    n = g * GROUP + t
                    src = bank[B_DOWN + t // 2][:, (t % 2) * D:(t % 2 + 1) * D]
                    ev["x2", n] = last_read[B_DOWN + t // 2] = dve.do(lambda e, n=n, src=src: e.tensor_tensor(
                        rb.row(n)[:], src, xr[n % 12][:], ALU.add), ev["down", g * KM + KM - 1],
                        ev["xr", n], rb.place_free(n), got("x2s", n - 2 * GROUP))
                    ev["x2s", n] = sp.dma(r_store, lambda e, n=n: e.dma_start(
                        late_rows[n * P:(n + 1) * P, :], rb.row(n)[:]), ev["x2", n])

            def when(first, n, step):
                return n >= first and (n - first) % step == 0 and (n - first) // step < (NT if step == 1 else NG)

            for n in range(3):
                load(n)
            for s in range(NT + 24):
                def on(k, f):
                    if 0 <= s - k < NT:
                        f(s - k)

                on(-3, load)
                on(2, norm_zn)
                on(6, norm_h)
                on(2, turn_zn)
                on(5, project)
                on(6, turn_h)
                on(3, lambda n: products(n, "k"))
                on(2, low_zn)
                on(6, low_h)
                on(5, residual)
                on(3, scores_t)
                on(2, qkv)
                on(4, lambda n: products(n, "v"))
                g, j = divmod(s - 10, GROUP)
                fc = 0 <= g < NG
                if fc:
                    up_mid(g, 2 * j)
                on(3, scores_back)
                on(2, feat)
                on(3, scale_scores)
                gp, jp = divmod(s - 11, GROUP)
                if 0 <= gp < NG:
                    down_mid(gp, 2 * jp + 1)
                if when(14, s, GROUP):
                    x2((s - 14) // GROUP)
                    g2 = (s - 14) // GROUP
                    rb.stats(g2, {n: ev["x2", n] for n in rb.tiles(g2)})
                on(4, attended)
                on(1, norm_z)
                on(0, stat_x)
                if fc:
                    up_mid(g, 2 * j + 1)
                    down_mid(g, 2 * j)
                on(4, low_o)
                for first in (15, 16):
                    if when(first, s, GROUP):
                        n0 = s - first + 2 * (first - 15)
                        for n in (n0, n0 + 1):
                            last_read[B_TURN] = rb.normed(n, bank[B_TURN], last_read[B_TURN])
                if when(17, s, GROUP):
                    rb.logits((s - 17) // GROUP, bank[B_S], last_read[B_S])
                    last_read[B_S] = rb.choose((s - 17) // GROUP)
                    rb.soften((s - 17) // GROUP)
                if when(18, s, GROUP):
                    rb.count((s - 18) // GROUP, bank[B_S], last_read[B_S])
                    last_read[B_S] = rb.dispatch((s - 18) // GROUP)
            done_mid = everything()

        for s in (dve, act, pool, sp, pe):
            s.wait(*done_mid)
        with ExitStack() as phase:
            ex_b = Experts(weight_buffers(phase, "b"))
            ex_b.allocate(phase, "xb")
            for x in range(2):
                for c in range(KE // 2):
                    ex_b.load_weights(x, c)
                    if x == 0:
                        ex_b.split_weights(x, c)
            ex_b.run(tables[1], late_rows, out_rows, done_mid, done_mid)

        sp.wait(*[v for r in rings for v in r.all()])

        block = ctx.enter_context(nc.Block())

        @block.sync
        def _(eng):
            sp.play(eng)

        @block.gpsimd
        def _(eng):
            pool.play(eng)

        @block.scalar
        def _(eng):
            act.play(eng)

        @block.vector
        def _(eng):
            dve.play(eng)

        @block.tensor
        def _(eng):
            pe.play(eng)


_INS = ["L0_attn_q_x", "L0_attn_ln1_w", "L0_attn_ln1_b", "L0_attn_wq", "L0_attn_bq", "L0_attn_wk", "L0_attn_bk",
        "L0_attn_wv", "L0_attn_bv", "L0_attn_wo", "L0_attn_bo", "L0_attn_ln2_w", "L0_attn_ln2_b", "L0_attn_fc_w",
        "L0_attn_fc_b", "L0_attn_proj_w", "L0_attn_proj_b", "L0_ffn_w_switch", "L0_ffn_b_switch", "L0_ffn_w1",
        "L0_ffn_b1", "L0_ffn_w2", "L0_ffn_b2"]
_OUTS = [((8, 512, 256), "float32")]


def kernel(**inputs):
    import numpy as _np
    import concourse.bacc as _bacc
    from concourse import mybir as _mybir
    from concourse.bass_utils import run_bass_kernel_spmd as _run

    nc = _bacc.Bacc("TRN2", target_bir_lowering=False, num_devices=1)
    arrays, args = {}, []
    for name in _INS:
        a = _np.ascontiguousarray(inputs[name])
        arrays[f"in_{name}_dram"] = a
        args.append(nc.dram_tensor(f"in_{name}_dram", a.shape, _mybir.dt.from_np(a.dtype), kind="ExternalInput").ap())
    for i, (shape, dtype) in enumerate(_OUTS):
        dt = _mybir.dt.from_np(_np.dtype(dtype))
        args.append(nc.dram_tensor(f"out_{i}_dram", shape, dt, kind="ExternalOutput").ap())
    build(nc, *args)
    r = _run(nc, [arrays], core_ids=[0])
    return r.results[0]["out_0_dram"]
```

```python
from contextlib import ExitStack

import concourse.bass as bass
from concourse import mybir

F32 = mybir.dt.float32
F32R = mybir.dt.float32r
BF16 = mybir.dt.bfloat16
I32 = mybir.dt.int32
ALU = mybir.AluOpType
ACT = mybir.ActivationFunctionType
AX = mybir.AxisListType.X

P = 128
GROUP = 4
EPS = 1e-5
ATTN_EPS = 1e-6
CAP_FACTOR = 0.5


class Stream:

    def __init__(self, sem):
        self.sem, self.count, self.queue, self.seen = sem, 0, [], {}

    def _waits(self, after):
        need = {}
        for event in after:
            if event is not None:
                sem, value = event
                if self.seen.get(id(sem), 0) < value:
                    self.seen[id(sem)] = value
                    need[id(sem)] = (sem, value)
        for sem, value in need.values():
            self.queue.append(lambda eng, sem=sem, value=value: eng.wait_ge(sem, value))

    def do(self, instruction, *after):
        self._waits(after)
        self.count += 1
        self.queue.append(lambda eng: instruction(eng).then_inc(self.sem, 1))
        return self.sem, self.count

    def quiet(self, instruction, *after):
        self._waits(after)
        self.queue.append(instruction)

    def dma(self, ring, transfer, *after):
        sem, value, before = ring.next()
        self._waits((*after, before))
        self.queue.append(lambda eng: transfer(eng).then_inc(sem, 16))
        return sem, value

    def wait(self, *after):
        self._waits(after)

    def play(self, eng):
        for step in self.queue:
            step(eng)


class Ring:

    def __init__(self, sems):
        self.sems, self.values, self.used = sems, [0] * len(sems), 0

    def next(self):
        i = self.used % len(self.sems)
        before = (self.sems[i], self.values[i]) if self.values[i] else None
        self.values[i] += 16
        self.used += 1
        return self.sems[i], self.values[i], before

    def all(self):
        return [(s, v) for s, v in zip(self.sems, self.values) if v]


def build(nc, x_in, ln1_w, ln1_b, wq, bq, wk, bk, wv, bv, wo, bo, ln2_w, ln2_b,
          fc_w, fc_b, proj_w, proj_b, w_switch, b_switch, w1, b1, w2, b2, out):
    B, N, D = x_in.shape
    T = B * N
    NT = T // P
    NG = NT // GROUP
    KD = D // P
    HEADS = 16
    HD = D // HEADS
    HID = fc_w.shape[1]
    KM = HID // P
    E = b_switch.shape[0]
    CAP = int(CAP_FACTOR * T / E)
    SLOTS = E * CAP
    ST = CAP // P
    EH = w1.shape[2]
    KE = EH // P
    GT = GROUP * P
    NOWHERE = 1 << 16
    assert KD == 2 and HEADS * HD == D and KE % 2 == 0 and ST == 2

    x_rows = x_in.rearrange("b n d -> (b n) d")
    out_rows = out.rearrange("b n d -> (b n) d")
    tables = [nc.dram_tensor(f"table{i}", [SLOTS, 2], F32).ap() for i in range(2)]
    mid_rows = nc.dram_tensor("mid_rows", [T, D], F32).ap()
    late_rows = nc.dram_tensor("late_rows", [T, D], F32).ap()

    with ExitStack() as ctx:
        def sem(name):
            return ctx.enter_context(nc.semaphore(name))

        def ring(name, n):
            return Ring([sem(f"{name}{i}") for i in range(n)])

        pe, dve, act, pool, sp = (Stream(sem(f"s_{n}")) for n in ("pe", "dve", "act", "pool", "sp"))
        rings = []

        def new_ring(name, n):
            rings.append(ring(name, n))
            return rings[-1]

        r_const = new_ring("d_const", 8)
        r_weight = new_ring("d_weight", 4)
        r_x = new_ring("d_x", 8)
        r_rows = new_ring("d_rows", 2)
        r_gather = new_ring("d_gather", 8)
        r_store = new_ring("d_store", 8)
        r_scatter = new_ring("d_scatter", 12)
        r_final = new_ring("d_final", 4)

        def tile(stack, name, shape, dt=F32):
            return stack.enter_context(nc.sbuf_tensor(name, shape, dt))

        bank = [ctx.enter_context(nc.psum_tensor(f"bank{i}", [P, 512], F32)) for i in range(8)]

        ident = tile(ctx, "ident", [P, P])
        upto = tile(ctx, "upto", [P, P], BF16)
        ones_bf = tile(ctx, "ones_bf", [P, P], BF16)
        ones_row = tile(ctx, "ones_row", [1, P])
        ones_two = tile(ctx, "ones_two", [2, P], F32R)
        token_id = tile(ctx, "token_id", [P, NT], I32)
        expert_i = tile(ctx, "expert_i", [P, GROUP, E], I32)
        first_wins = tile(ctx, "first_wins", [P, GROUP, E])
        switch_w = tile(ctx, "switch_w", [P, KD, E])
        switch_b = tile(ctx, "switch_b", [1, GROUP, E])
        col_rows = E * KE + KM + 4 * KD
        cols = tile(ctx, "cols", [P, col_rows])
        C_FCB = E * KE
        C_LN = C_FCB + KM
        BO, PB = 3 * D, 4 * D
        BIASES = 5 + E
        bias_rows = tile(ctx, "bias_rows", [2, BIASES * D], F32R)
        seen_sum = tile(ctx, "seen_sum", [P, 2, E], BF16)
        minus_half = tile(ctx, "minus_half", [P, GROUP])
        e_mh = pool.do(lambda e: e.memset(minus_half[:], -0.5))

        with ExitStack() as once:
            col_src = tile(once, "col_src", [col_rows, P])
            bias_raw = tile(once, "bias_raw", [BIASES, D])
            bias_parts = [tile(once, f"bias_part{i}", [BIASES, D], F32R) for i in range(2)]
            blank = tile(once, "blank", [P, SLOTS // P, 2])

        qkv_w = [tile(ctx, f"qkv_w{i}", [P, KD, 3 * D], F32R) for i in range(2)]
        o_w = [tile(ctx, f"o_w{i}", [P, KD, D], F32R) for i in range(2)]
        up_w = [tile(ctx, f"up_w{i}", [P, KD, HID], F32R) for i in range(2)]
        down_w = [tile(ctx, f"down_w{i}", [P, KM, D], F32R) for i in range(2)]

        def f32(ap):
            return ap.bitcast(F32)

        def product(dst, left, right, first, last, *after, signal=True):
            (lh, ll), (rh, rl) = left, right
            pe.quiet(lambda e: e.matmul(dst, lh, rh, start=first, stop=False, skip_group_check=True), *after)
            pe.quiet(lambda e: e.matmul(dst, lh, rl, start=False, stop=False, skip_group_check=True))
            go = pe.do if signal else pe.quiet
            return go(lambda e: e.matmul(dst, ll, rh, start=False, stop=last, skip_group_check=True))

        def add_bias(dst, rows, first, *after):
            pe.quiet(lambda e: e.matmul(dst, ones_two[:, 0:P], rows, start=first, stop=False,
                                        skip_group_check=True), *after)

        def turn(dst, src, *after, start=True, stop=True, signal=True):
            go = pe.do if signal else pe.quiet
            return go(lambda e: e.matmul(dst, src, ident[:], is_transpose=True, start=start, stop=stop,
                                         skip_group_check=True), *after)

        e_ident0 = pool.do(lambda e: e.memset(ident[:], 0.0))
        e_upto0 = pool.do(lambda e: e.memset(upto[:], 1.0))
        e_blank0 = pool.do(lambda e: e.memset(blank[:], 0.0))
        e_ident = pool.do(lambda e: e.affine_select(
            out=ident[:], in_=ident[:], compare_op=ALU.not_equal, fill=1.0, base=0,
            pattern=[[-1, P]], channel_multiplier=1), e_ident0)
        e_upto = pool.do(lambda e: e.affine_select(
            out=upto[:], in_=upto[:], compare_op=ALU.is_ge, fill=0.0, base=0,
            pattern=[[1, P]], channel_multiplier=-1), e_upto0)
        e_blank = pool.do(lambda e: e.memset(blank[:, :, 0].bitcast(I32), NOWHERE), e_blank0)
        e_ids = pool.do(lambda e: e.iota(token_id[:], pattern=[[P, NT]], base=0, channel_multiplier=1))
        e_iota = pool.do(lambda e: e.iota(expert_i[:], pattern=[[0, GROUP], [-1, E]], base=E, channel_multiplier=0))
        e_ones = dve.do(lambda e: e.memset(ones_bf[:], 1.0))
        dve.do(lambda e: e.memset(ones_row[:], 1.0))
        dve.do(lambda e: e.memset(f32(ones_two[:]), 1.0))
        dve.do(lambda e: e.memset(seen_sum[:], 0.0))
        e_consts = dve.do(lambda e: e.tensor_copy(first_wins[:], expert_i[:]), e_iota)

        def load_router():
            nonlocal e_sw, e_sb
            e_sw = sp.dma(r_const, lambda e: e.dma_start(switch_w[:], w_switch.rearrange("(k p) e -> p k e", p=P)))
            e_sb = sp.dma(r_const, lambda e: e.dma_start(
                switch_b[:], b_switch.unsqueeze(0).unsqueeze(0).broadcast_to([1, GROUP, E])))

        def load_biases():
            col_parts = [(b1.rearrange("e (m p) -> (e m) p", p=P), E * KE), (fc_b.rearrange("(m p) -> m p", p=P), KM)]
            col_parts += [(v.rearrange("(m p) -> m p", p=P), KD) for v in (ln1_w, ln1_b, ln2_w, ln2_b)]
            at = 0
            for src, n in col_parts:
                e_cols.append(sp.dma(r_const, lambda e, src=src, at=at, n=n: e.dma_start(col_src[at:at + n, :], src)))
                at += n
            for i, v in enumerate((bq, bk, bv, bo, proj_b)):
                e_brow.append(sp.dma(r_const, lambda e, i=i, v=v: e.dma_start(bias_raw[i:i + 1, :], v.unsqueeze(0))))
            e_brow.append(sp.dma(r_const, lambda e: e.dma_start(bias_raw[5:5 + E, :], b2)))

        def turn_biases(dst):
            e = pe.do(lambda e: e.matmul(dst[:, 0:col_rows], col_src[:], ident[0:col_rows, 0:col_rows],
                                         is_transpose=True, start=True, stop=True), e_ident, *e_cols)
            return act.do(lambda e: e.copy(cols[:], dst[:, 0:col_rows]), e)

        def split_biases():
            high, low = bias_parts
            e = dve.do(lambda e: e.tensor_copy(high[:], bias_raw[:]), *e_brow)
            a = dve.do(lambda e: e.tensor_tensor(low[:], bias_raw[:], f32(high[:]), ALU.subtract), e)
            for i, part in enumerate(bias_parts):
                sp.dma(r_const, lambda e, i=i, part=part: e.dma_start(
                    f32(bias_rows[i:i + 1, :]).rearrange("o (b d) -> o b d", b=BIASES), f32(part[:])), a)

        e_sw = e_sb = None
        e_cols, e_brow, e_blank_rows = [], [], []

        def blank_table(i):
            e_blank_rows.append(sp.dma(r_store, lambda e: e.dma_start(
                tables[i].rearrange("(p c) r -> p c r", p=P), blank[:]), e_blank))

        class Router:

            def __init__(self, stack, name, depth, unit_depth, feat_depth, table, passed):
                self.table, self.passed, self.depth, self.unit_depth = table, passed, depth, unit_depth
                self.plain = tile(stack, f"{name}_plain", [P, depth, D])
                self.unit = [tile(stack, f"{name}_unit{i}", [P, D]) for i in range(self.unit_depth)]
                self.feat = [tile(stack, f"{name}_feat{i}", [P, KD, P]) for i in range(feat_depth)]
                self.stat = [tile(stack, f"{name}_stat{i}", [P, GROUP, 6]) for i in range(2)]
                self.mean_var = [tile(stack, f"{name}_mv{i}", [P, GROUP, 2]) for i in range(2)]
                self.rstd = [tile(stack, f"{name}_rstd{i}", [P, GROUP]) for i in range(2)]
                self.shift = [tile(stack, f"{name}_shift{i}", [P, GROUP]) for i in range(2)]
                self.result = [tile(stack, f"{name}_pass{i}", [P, D]) for i in range(GROUP)]
                self.tmp = tile(stack, f"{name}_tmp", [P, GROUP, E])
                self.hot = [tile(stack, f"{name}_hot{i}", [P, GROUP, E], BF16) for i in range(2)]
                self.ex = [tile(stack, f"{name}_ex{i}", [P, GROUP, E]) for i in range(2)]
                self.recent = tile(stack, f"{name}_recent", [P, E])
                self.best = [tile(stack, f"{name}_best{i}", [P, 2, GROUP]) for i in range(2)]
                self.small = tile(stack, f"{name}_small", [P, 6, GROUP])
                self.entry = [tile(stack, f"{name}_entry{i}", [P, GROUP, 2]) for i in range(2)]
                self.dest = [tile(stack, f"{name}_dest{i}", [P, GROUP], I32) for i in range(2)]
                self.sent, self.stored, self.norm, self.featd, self.logits_done = {}, {}, {}, {}, {}
                self.hot_ready, self.exped, self.counted, self.chosen, self.dispatched = {}, {}, {}, {}, {}
                self.result_made, self.std, self.shifted = {}, {}, {}
                self.seen_ready = None

            def row(self, n):
                return self.plain[:, n % self.depth]

            def place_free(self, n):
                return self.result_made.get(n - self.depth)

            def tiles(self, g):
                return range(g * GROUP, (g + 1) * GROUP)

            def stats(self, g, ready):
                st, mv = self.stat[g % 2], self.mean_var[g % 2]
                es = [dve.do(lambda e, i=i, n=n: e.bn_stats(st[:, i], self.row(n)), ready[n])
                      for i, n in enumerate(self.tiles(g))]
                es = [dve.do(lambda e, i=i: e.bn_aggr(mv[:, i], st[:, i]), es[i], self.norm.get((g - 1) * GROUP - 1))
                      for i in range(GROUP)]
                self.spread = es

            def roots(self, g):
                mv, rs = self.mean_var[g % 2], self.rstd[g % 2]
                e = pool.do(lambda e: e.tensor_scalar(rs[:], mv[:, :, 1], EPS, None, ALU.add), *self.spread,
                            self.norm.get((g - 1) * GROUP - 1))
                self.std[g] = pool.do(lambda e: e.tensor_tensor(rs[:], rs[:], minus_half[:], ALU.pow), e)

            def shifts(self, g):
                mv, rs, shift = self.mean_var[g % 2], self.rstd[g % 2], self.shift[g % 2]
                self.shifted[g] = dve.do(lambda e: e.scalar_tensor_tensor(
                    out=shift[:], in0=mv[:, :, 0], scalar=-1.0, in1=rs[:], op0=ALU.mult, op1=ALU.mult), self.std[g],
                    self.norm.get((g - 1) * GROUP - 1))

            def normed(self, n):
                g, i = divmod(n, GROUP)
                rs, shift, row = self.rstd[g % 2], self.shift[g % 2], self.row(n)
                unit = self.unit[n % self.unit_depth]
                self.norm[n] = act.do(lambda e: e.activation(
                    unit[:], row, ACT.Identity, bias=shift[:, i:i + 1], scale=rs[:, i:i + 1]),
                    self.shifted[g], self.result_made.get(n - self.unit_depth))

            def turned(self, n, dst, *bank_free):
                feat, unit = self.feat[n % len(self.feat)], self.unit[n % self.unit_depth]
                for k in range(KD):
                    e = turn(dst[:, k * P:(k + 1) * P], unit[:, k * P:(k + 1) * P], self.norm[n], *bank_free,
                             signal=k == KD - 1)
                self.featd[n] = act.do(lambda e: e.copy(feat[:], dst[:, 0:D].rearrange("p (k t) -> p k t", k=KD)),
                                       e, self.logits_done.get((n - len(self.feat)) // GROUP))
                return self.featd[n]

            def logits(self, n, dst, *bank_free):
                g, i = divmod(n, GROUP)
                self.dst = dst = dst[:, 0:GROUP * E].rearrange("p (t e) -> p t e", t=GROUP)
                if i == 0:
                    pe.quiet(lambda e: e.matmul(dst, ones_row[:], switch_b[:], start=True, stop=False,
                                                skip_group_check=True), *bank_free)
                feat = self.feat[n % len(self.feat)]
                for k in range(KD):
                    self.logits_done[g] = pe.do(lambda e, k=k: e.matmul(
                        dst[:, i], feat[:, k], switch_w[:, k], start=False, stop=k == KD - 1,
                        skip_group_check=True), self.featd[n])

            def choose(self, g):
                src, best, wide = self.dst, self.best[g % 2], [P, GROUP, E]
                hot, ex = self.hot[g % 2], self.ex[g % 2]
                e_max = dve.do(lambda e: e.tensor_reduce(best[:, 0], src, AX, ALU.max), self.logits_done[g],
                               self.dispatched.get(g - 2))
                e = dve.do(lambda e: e.tensor_tensor(
                    self.tmp[:], src, best[:, 0].unsqueeze(2).broadcast_to(wide), ALU.is_ge), e_max,
                    self.dispatched.get(g - 1))
                e_sub = dve.do(lambda e: e.tensor_tensor(
                    ex[:], src, best[:, 0].unsqueeze(2).broadcast_to(wide), ALU.subtract), e_max)
                e = dve.do(lambda e: e.tensor_tensor(self.tmp[:], self.tmp[:], first_wins[:], ALU.mult), e)
                e = dve.do(lambda e: e.tensor_reduce(best[:, 1], self.tmp[:], AX, ALU.max), e)
                self.hot_ready[g] = self.chosen[g] = dve.do(lambda e: e.tensor_tensor(
                    hot[:], first_wins[:], best[:, 1].unsqueeze(2).broadcast_to(wide), ALU.is_equal), e)
                self.minus_max = e_sub
                return e_sub

            def soften(self, g):
                ex = self.ex[g % 2]
                self.exped[g] = act.do(lambda e: e.activation(ex[:], ex[:], ACT.Exp), self.minus_max)

            def count(self, g, dst, *bank_free):
                self.cdst = dst = dst[:, 0:GROUP * E].rearrange("p (t e) -> p t e", t=GROUP)
                hot = self.hot[g % 2]
                pe.quiet(lambda e: e.matmul(dst, upto[:], hot[:], start=True, stop=False, skip_group_check=True),
                         self.hot_ready[g], *bank_free)
                for j in range(GROUP - 1):
                    pe.quiet(lambda e, j=j: e.matmul(
                        dst[:, j + 1:], ones_bf[:], hot[:, j:j + 1].broadcast_to([P, GROUP - 1 - j, E]), start=False,
                        stop=False, skip_group_check=True))
                e = pe.do(lambda e: e.matmul(
                    dst, ones_bf[:], seen_sum[:, g % 2:g % 2 + 1].broadcast_to([P, GROUP, E]), start=False, stop=True,
                    skip_group_check=True), self.seen_ready)
                self.counted[g] = e
                if g + 1 < NG:
                    e = dve.do(lambda e: e.tensor_reduce(
                        self.recent[:], hot[:].rearrange("p t e -> p e t"), AX, ALU.add), self.hot_ready[g],
                        self.seen_ready)
                    self.seen_ready = dve.do(lambda e: e.tensor_tensor(
                        seen_sum[:, (g + 1) % 2], self.recent[:], seen_sum[:, g % 2], ALU.add), e,
                        self.counted.get(g - 1))

            def dispatch(self, g):
                src, sm, dest, best = self.cdst, self.small, self.dest[g % 2], self.best[g % 2]
                hot, ex, entry = self.hot[g % 2], self.ex[g % 2], self.entry[g % 2]
                entries_free = [v.get(n) for n in self.tiles(g - 2) for v in (self.sent, self.result_made)]
                e_read = dve.do(lambda e: e.tensor_tensor(self.tmp[:], src, hot[:], ALU.mult), self.counted[g],
                                self.chosen[g])
                e_s = dve.do(lambda e: e.tensor_reduce(sm[:, 3], ex[:], AX, ALU.add), self.exped[g],
                             self.dispatched.get(g - 1))
                e1 = dve.do(lambda e: e.tensor_reduce(sm[:, 0], self.tmp[:], AX, ALU.add), e_read)
                e_s = dve.do(lambda e: e.reciprocal(sm[:, 4], sm[:, 3]), e_s)
                e2 = dve.do(lambda e: e.tensor_scalar(sm[:, 1], sm[:, 0], float(CAP), float(NOWHERE), ALU.is_gt,
                                                      ALU.mult), e1)
                e3 = dve.do(lambda e: e.scalar_tensor_tensor(out=sm[:, 2], in0=best[:, 1], scalar=float(-CAP),
                                                             in1=sm[:, 0], op0=ALU.mult, op1=ALU.add), e1)
                e_s = dve.do(lambda e: e.reciprocal(sm[:, 5], sm[:, 4]), e_s)
                e_dest = dve.do(lambda e: e.scalar_tensor_tensor(
                    out=dest[:], in0=sm[:, 2], scalar=float(CAP * E - 1), in1=sm[:, 1], op0=ALU.add, op1=ALU.add),
                    e2, e3, *entries_free)
                e_scale = dve.do(lambda e: e.scalar_tensor_tensor(
                    out=entry[:, :, 1], in0=sm[:, 4], scalar=0.5, in1=sm[:, 5], op0=ALU.mult, op1=ALU.mult), e_s,
                    *entries_free)
                e_id = act.do(lambda e: e.copy(entry[:, :, 0].bitcast(I32), token_id[:, g * GROUP:(g + 1) * GROUP]),
                              *entries_free)
                self.dispatched[g] = e_scale
                self.entries_made = (e_id, e_scale, e_dest)
                return e_read

            def send(self, n):
                g, i = divmod(n, GROUP)
                dest, entry = self.dest[g % 2], self.entry[g % 2]
                row, unit, res = self.row(n), self.unit[n % self.unit_depth], self.result[n % len(self.result)]
                self.sent[n] = pool.dma(r_scatter, lambda e: e.indirect_dma_start(
                    self.table, bass.IndirectOffsetOnAxis(ap=dest[:, i:i + 1], axis=0), entry[:, i], None,
                    bounds_check=SLOTS - 1, oob_is_err=False), *self.entries_made, *e_blank_rows)
                e = dve.do(lambda e: e.scalar_tensor_tensor(
                    out=res[:], in0=unit[:], scalar=entry[:, i, 1:2], in1=row, op0=ALU.mult,
                    op1=ALU.add), self.entries_made[1], self.norm[n], self.stored.get(n - len(self.result)))
                self.stored[n] = sp.dma(r_store, lambda e: e.dma_start(self.passed[n * P:(n + 1) * P, :], res[:]), e)
                self.result_made[n] = e

        class Experts:

            def __init__(self, bufs):
                self.raw, self.w1s, self.w2s = bufs
                self.got, self.split, self.up_done, self.down_done = {}, {}, {}, {}

            def allocate(self, stack, name):
                self.table = tile(stack, f"{name}_table", [P, E * ST, 2])
                self.token = tile(stack, f"{name}_token", [P, E * ST], I32)
                self.rows = [tile(stack, f"{name}_rows{i}", [P, ST, D]) for i in range(3)]
                self.unit = [tile(stack, f"{name}_unit{i}", [P, ST, D]) for i in range(2)]
                self.stat = [tile(stack, f"{name}_stat{i}", [P, ST, 6]) for i in range(2)]
                self.mean_var = [tile(stack, f"{name}_mv{i}", [P, ST, 2]) for i in range(2)]
                self.rstd = [tile(stack, f"{name}_rstd{i}", [P, ST]) for i in range(2)]
                self.xt = tile(stack, f"{name}_xt", [P, KD, CAP])
                self.xts = [[tile(stack, f"{name}_xt{b}{i}", [P, KD, CAP], F32R) for i in range(2)] for b in range(2)]
                self.h = [tile(stack, f"{name}_h{i}", [P, 2, CAP]) for i in range(2)]
                self.hs = [[tile(stack, f"{name}_h{b}{i}", [P, 2, CAP], F32R) for i in range(2)] for b in range(4)]
                self.fin = [tile(stack, f"{name}_fin{i}", [P, D]) for i in range(4)]

            def load_weights(self, x, c):
                r1, r2 = self.raw
                free = self.split.get((x - 1, c), (None, None))
                a, b = c * 2 * P, (c + 1) * 2 * P
                self.got[x, c] = (
                    sp.dma(r_weight, lambda e: e.dma_start(
                        r1[:, :, a:b], w1[x, :, a:b].rearrange("(k p) n -> p k n", p=P)), free[0]),
                    sp.dma(r_weight, lambda e: e.dma_start(
                        r2[:, 2 * c:2 * c + 2], w2[x, a:b].rearrange("(k p) n -> p k n", p=P)), free[1]))

            def split_weights(self, x, c, low_engine=pool):
                r1, r2 = self.raw
                (h1, l1), (h2, l2) = self.w1s[x % 2], self.w2s[x % 2]
                cut1, cut2 = (slice(None), slice(None), slice(c * 2 * P, (c + 1) * 2 * P)), (slice(None), slice(2 * c, 2 * c + 2))
                got1, got2 = self.got[x, c]
                u = (x - 2) * KE // 2 + c
                e = dve.do(lambda e: e.tensor_copy(h1[cut1], r1[cut1]), got1, self.up_done.get(u))
                e1 = dve.do(lambda e: e.tensor_tensor(l1[cut1], r1[cut1], f32(h1[cut1]), ALU.subtract), e)
                e = act.do(lambda e: e.copy(h2[cut2], r2[cut2]), got2, self.down_done.get(u))
                e2 = low_engine.do(lambda e: e.tensor_tensor(l2[cut2], r2[cut2], f32(h2[cut2]), ALU.subtract), e)
                self.split[x, c] = (e1, e2)

            def run(self, slot_table, source, target, arrived, passed, between=None):
                split, up_done, down_done = self.split, self.up_done, self.down_done
                got_rows, normed, turned, xt_ready, fin_read = {}, {}, {}, {}, {}
                fin_sent = {}
                table, token = self.table, self.token
                e_table = sp.dma(r_rows, lambda e: e.dma_start(
                    table[:], slot_table.rearrange("(c p) r -> p c r", p=P)), *arrived)
                e_token = dve.do(lambda e: e.tensor_scalar(token[:], table[:, :, 0].bitcast(I32), T - 1, None,
                                                           ALU.min), e_table)

                def load_rows(x):
                    buf = self.rows[x % 3]
                    got_rows[x] = [pool.dma(r_gather, lambda e, s=s: e.indirect_dma_start(
                        buf[:, s], None, source,
                        bass.IndirectOffsetOnAxis(ap=token[:, x * ST + s:x * ST + s + 1], axis=0)),
                        e_token, *arrived, *fin_read.get(x - 3, ())) for s in range(ST)]

                def norm_rows(x):
                    buf, unit = self.rows[x % 3], self.unit[x % 2]
                    st, mv, rs = self.stat[x % 2], self.mean_var[x % 2], self.rstd[x % 2]
                    es = [dve.do(lambda e, s=s: e.bn_stats(st[:, s], buf[:, s]), got_rows[x][s]) for s in range(ST)]
                    es = [dve.do(lambda e, s=s: e.bn_aggr(mv[:, s], st[:, s]), es[s]) for s in range(ST)]
                    e = pool.do(lambda e: e.tensor_scalar(rs[:], mv[:, :, 1], EPS, None, ALU.add), *es,
                                *normed.get(x - 2, ()))
                    e = pool.do(lambda e: e.tensor_tensor(rs[:], rs[:], minus_half[:, 0:ST], ALU.pow), e)
                    normed[x] = [dve.do(lambda e, s=s: e.tensor_scalar(
                        unit[:, s], buf[:, s], mv[:, s, 0:1], rs[:, s:s + 1], ALU.subtract, ALU.mult),
                        es[s], e, turned.get(x - 2)) for s in range(ST)]

                def turn_rows(x):
                    unit = self.unit[x % 2]
                    dst = bank[4]
                    for k in range(KD):
                        for s in range(ST):
                            e = turn(dst[:, k * CAP + s * P:k * CAP + (s + 1) * P], unit[:, s, k * P:(k + 1) * P],
                                     normed[x][s], xt_ready.get(x - 1), signal=(k, s) == (KD - 1, ST - 1))
                    turned[x] = e
                    src = dst[:].rearrange("p (k c) -> p k c", k=KD)
                    hi, lo = self.xts[x % 2]
                    a = act.do(lambda e: e.copy(self.xt[:], src), e, xt_lo.get(x - 1))
                    b = act.do(lambda e: e.copy(hi[:], src), e, up_done.get((x - 1) * pairs - 1))
                    xt_lo[x] = dve.do(lambda e: e.tensor_tensor(lo[:], self.xt[:], f32(hi[:]), ALU.subtract), a, b)
                    xt_ready[x] = b

                xt_lo = {}
                pairs = KE // 2

                def up(x, j):
                    u = x * pairs + j
                    dst = bank[u % 2]
                    hi, lo = self.w1s[x % 2]
                    xh, xl = self.xts[x % 2]
                    for i in range(2):
                        m = 2 * j + i
                        for k in range(KD):
                            e = product(dst[:, i * CAP:(i + 1) * CAP],
                                        (hi[:, k, m * P:(m + 1) * P], lo[:, k, m * P:(m + 1) * P]),
                                        (xh[:, k], xl[:, k]), k == 0, k == KD - 1,
                                        xt_lo[x], split[x, j][0], h_read.get(u - 2), signal=k == KD - 1)
                    up_done[u] = e
                    h32 = self.h[u % 2]
                    hh, hl = self.hs[u % 4]
                    for i in range(2):
                        m = 2 * j + i
                        a = act.do(lambda e, i=i, m=m: e.activation(
                            h32[:, i], dst[:, i * CAP:(i + 1) * CAP], ACT.Relu,
                            bias=cols[:, x * KE + m:x * KE + m + 1]), e, h_lo.get(u - 2))
                        a = act.do(lambda e, i=i, m=m: e.activation(
                            hh[:, i], dst[:, i * CAP:(i + 1) * CAP], ACT.Relu,
                            bias=cols[:, x * KE + m:x * KE + m + 1]), down_done.get(u - 4))
                    h_read[u] = a
                    h_lo[u] = dve.do(lambda e: e.tensor_tensor(hl[:], h32[:], f32(hh[:]), ALU.subtract), a)

                h_read, h_lo = {}, {}

                def down(x, j):
                    u = x * pairs + j
                    dst = bank[2 + x % 2]
                    hi, lo = self.w2s[x % 2]
                    hh, hl = self.hs[u % 4]
                    if j == 0:
                        for s in range(ST):
                            add_bias(dst[:, s * D:(s + 1) * D], bias_rows[:, (5 + x) * D:(6 + x) * D], s == 0,
                                     *fin_read.get(x - 2, ()))
                    for i in range(2):
                        m = 2 * j + i
                        for s in range(ST):
                            e = product(dst[:, s * D:(s + 1) * D],
                                        (hh[:, i, s * P:(s + 1) * P], hl[:, i, s * P:(s + 1) * P]),
                                        (hi[:, m], lo[:, m]), False, m == KE - 1, h_lo[u], split[x, j][1],
                                        signal=(i, s) == (1, ST - 1))
                    down_done[u] = e
                    if j == pairs - 1:
                        finish(x, e)

                def finish(x, e_y):
                    dst, buf = bank[2 + x % 2], self.rows[x % 3]
                    reads = []
                    for s in range(ST):
                        f, c = self.fin[(x * ST + s) % 4], x * ST + s
                        e = dve.do(lambda e, s=s, f=f, c=c: e.scalar_tensor_tensor(
                            out=f[:], in0=dst[:, s * D:(s + 1) * D], scalar=table[:, c, 1:2],
                            in1=buf[:, s], op0=ALU.mult, op1=ALU.add), e_y, fin_sent.get(c - 4))
                        fin_sent[c] = pool.dma(r_scatter, lambda e, s=s, f=f, c=c: e.indirect_dma_start(
                            target, bass.IndirectOffsetOnAxis(ap=table[:, c, 0:1].bitcast(I32), axis=0),
                            f[:], None, bounds_check=T - 1, oob_is_err=False), e, *passed)
                        reads.append(e)
                    fin_read[x] = reads

                lag = 2
                load_rows(0)
                norm_rows(0)
                turn_rows(0)
                load_rows(1)
                load_rows(2)
                for u in range(E * pairs + lag):
                    x, j = divmod(u, pairs)
                    if x < E:
                        up(x, j)
                        if j == 0 and x + 1 < E:
                            norm_rows(x + 1)
                        if j == 2 and x + 1 < E:
                            turn_rows(x + 1)
                    if u >= lag:
                        px, pj = divmod(u - lag, pairs)
                        down(px, pj)
                        if pj == pairs - 1 and px + 3 < E:
                            load_rows(px + 3)
                    if x + 1 < E:
                        self.split_weights(x + 1, j)
                    if x + 2 < E:
                        self.load_weights(x + 2, j)
                    if x < E and between:
                        between(u)
                return [v for v in fin_sent.values()] + [(s.sem, s.count) for s in (pe, dve, act)]

        def weight_buffers(stack, name):
            raw = [tile(stack, f"{name}_raw{w}", [P, *shape]) for w, shape in enumerate(((KD, EH), (KE, D)))]
            even, odd = ([[tile(stack, f"{name}_w{b}{w}{i}", [P, *shape], F32R) for i in range(2)]
                          for w, shape in enumerate(((KD, EH), (KE, D)))] for b in range(2))
            return raw, [even[0], odd[0]], [even[1], odd[1]]

        def so_far(streams=(pe, dve, act, pool)):
            return [(s.sem, s.count) for s in streams]

        def everything():
            return so_far() + [v for r in rings for v in r.all()]

        with ExitStack() as phase:
            ex_a = Experts(weight_buffers(phase, "a"))
            ex_a.allocate(phase, "xa")
            piece_raw = [tile(phase, f"piece_raw{i}", [P, KM * D]) for i in range(2)]
        with ExitStack() as phase:
            tile(phase, "below_router", [P, 3 * (KD * EH + KE * D)])
            ra = Router(phase, "ra", 6 * GROUP, 3 * GROUP, 2 * GROUP, tables[0], mid_rows)
        ra.seen_ready = e_consts
        loaded = {}

        def load_x(n0, n):
            at = n0 % ra.depth
            e = sp.dma(r_x, lambda e: e.dma_start(
                ra.plain[:, at:at + n], x_rows[n0 * P:(n0 + n) * P, :].rearrange("(t p) d -> p t d", p=P)),
                ra.place_free(n0 + n - 1))
            loaded.update({n0 + i: e for i in range(n)})

        for n in range(GROUP):
            load_x(n, 1)
        load_router()
        for g in range(1, 3):
            load_x(g * GROUP, GROUP)
        blank_table(0)
        load_biases()
        for g in range(3, 6):
            load_x(g * GROUP, GROUP)
        for c in range(KE // 2):
            ex_a.load_weights(0, c)
        blank_table(1)
        pe.wait(e_ident, e_upto, e_ones, e_consts, e_mh, e_sw, e_sb)
        act.wait(e_ids)
        bank_free = [None] * 8
        for g in range(NG + 3):
            if 2 <= g < NG + 2:
                for n in ra.tiles(g - 2):
                    ra.logits(n, bank[6], bank_free[6])
            if 1 <= g <= NG:
                ra.shifts(g - 1)
                for n in ra.tiles(g - 1):
                    ra.normed(n)
                for n in ra.tiles(g - 1):
                    bank_free[n % 4] = ra.turned(n, bank[n % 4], bank_free[n % 4])
            if g < NG:
                ra.stats(g, loaded)
                ra.roots(g)
            if g >= 3:
                bank_free[7] = ra.dispatch(g - 3)
                for n in ra.tiles(g - 3):
                    ra.send(n)
                if g + 3 < NG:
                    load_x((g + 3) * GROUP, GROUP)
            if 2 <= g < NG + 2:
                bank_free[6] = ra.choose(g - 2)
                ra.soften(g - 2)
                ra.count(g - 2, bank[7], bank_free[7])
            if g == 1:
                bank_free[5] = turn_biases(bank[5])
            if g == 2:
                split_biases()
            if 2 <= g < 2 + KE // 2:
                ex_a.split_weights(0, g - 2, pool if g < 4 else dve)
                ex_a.load_weights(1, g - 2)
        arrived = everything()

        for s in (dve, act, pool, pe, sp):
            s.wait(*arrived)
        pieces = [
            (qkv_w, KD, [(wq, 0, D), (wk, D, D), (wv, 2 * D, D)]),
            (o_w, KD, [(wo, 0, D)]),
            (up_w, KD, [(fc_w, 0, HID)]),
            (down_w, KM, [(proj_w, 0, D)]),
        ]

        chunks = [(i, k, c) for i, (_, n, parts) in enumerate(pieces) for k in range(n)
                  for c in range(0, parts[-1][1] + parts[-1][2], D)]
        piece_got, piece_read = {}, {}
        late = 4

        def piece_view(i):
            _, n, parts = pieces[i]
            return piece_raw[i % 2][:, 0:n * (parts[-1][1] + parts[-1][2])].rearrange("p (k n) -> p k n", k=n)

        def load_piece(i):
            view = piece_view(i)
            piece_got[i] = [sp.dma(r_weight, lambda e, w=w, c=c, n=n: e.dma_start(
                view[:, :, c:c + n], w.rearrange("(k p) n -> p k n", p=P)), piece_read.get(i - 2))
                for w, c, n in pieces[i][2]]

        def middle_weights(u):
            if u == 0:
                load_piece(0)
                load_piece(1)
            elif late <= u < late + len(chunks):
                i, k, c = chunks[u - late]
                view, (high, low) = piece_view(i), pieces[i][0]
                e = act.do(lambda e: e.copy(high[:, k, c:c + D], view[:, k, c:c + D]), *piece_got[i])
                piece_read[i] = dve.do(lambda e: e.tensor_tensor(
                    low[:, k, c:c + D], view[:, k, c:c + D], f32(high[:, k, c:c + D]), ALU.subtract), e)
                if i + 2 < len(pieces) and chunks[u - late + 1][0] != i:
                    load_piece(i + 2)

        ex_a.run(tables[0], x_rows, mid_rows, arrived, arrived, middle_weights)
        done_a = everything()

        for s in (dve, act, pool, sp, pe):
            s.wait(*done_a)
        with ExitStack() as mid:
            def many(name, n, shape, dt=F32):
                return [tile(mid, f"{name}{i}", shape, dt) for i in range(n)]

            prod_ = many("prod_", 8, [P, 4, D])
            feats = many("feats_", 2, [P, 2 * D])
            soft = many("soft_", 1, [P, 2 * D])
            vals = many("vals_", 3, [P, D])
            stt = many("stt_", 1, [P, D])
            score = many("score_", 2, [P, D])
            xnt = many("xnt_", 1, [P, KD, P])
            xnts = [many(f"xnts{i}_", 2, [P, KD, P], F32R) for i in range(2)]
            scrap = many("scrap", 1, [P, 1])[0]
            ssum = many("ssum_", 2, [P, 2, HEADS])
            x1 = many("x1_", 8, [P, D])
            z = many("z_", 5, [P, D])
            zn = many("zn_", 2, [P, D])
            stz = many("stz_", 3, [P, 10])
            stn = many("stn_", 3, [P, 10])
            sth = many("sth_", 3, [P, 10])
            ot = many("ot_", 1, [P, D])
            ots = [many(f"ots{i}_", 2, [P, D], F32R) for i in range(2)]
            xa = many("xa_", 3, [P, D])
            xr = many("xr_", 10, [P, D])
            hn = many("hn_", 2, [P, D])
            hnt = many("hnt_", 1, [P, KD, P])
            hnts = [many(f"hnts{i}_", 2, [P, KD, GT], F32R) for i in range(2)]
            hid = many("hid_", 2, [P, GT])
            hids = [many(f"hids{i}_", 3, [P, GT], F32R) for i in range(2)]
            rb = Router(mid, "rb", 2 * GROUP, 2 * GROUP, GROUP, tables[1], out_rows)
            rb.seen_ready = dve.do(lambda e: e.memset(seen_sum[:, 0], 0.0))

        with ExitStack() as phase:
            ex_b = Experts(weight_buffers(phase, "b"))
            ex_b.allocate(phase, "xb")
        B_TURN, B_QK, B_V, B_ACC, B_S, B_UP, B_DOWN = 0, 1, 2, 3, 4, 5, 6

        ev = {}

        def got(*key):
            return ev.get(key)

        last_read = {i: None for i in range(8)}

        def rstd(st, key):
            e = dve.do(lambda e: e.bn_aggr(st[:, 6:8], st[:, 0:6]), ev[("bn", *key)])
            e = pool.do(lambda e: e.tensor_scalar(st[:, 7:8], st[:, 7:8], EPS, None, ALU.add), e)
            ev[key] = pool.do(lambda e: e.tensor_tensor(st[:, 8:9], st[:, 7:8], minus_half[:, 0:1], ALU.pow), e)

        def load(n):
            ev["x1", n] = sp.dma(r_x, lambda e: e.dma_start(x1[n % 8][:], mid_rows[n * P:(n + 1) * P, :]),
                                 got("xr", n - 8), got("z", n - 8))

        def stat_x(n):
            st = stz[n % 3]
            ev["bn", "stz", n] = dve.do(lambda e: e.bn_stats(st[:, 0:6], x1[n % 8][:]), got("x1", n),
                                        got("z", n - 3))

        def norm_z(n):
            st = stz[n % 3]
            ev["z", n] = dve.do(lambda e: e.tensor_scalar(
                z[n % 5][:], x1[n % 8][:], st[:, 6:7], st[:, 8:9], ALU.subtract, ALU.mult),
                got("stz", n), got("xa", n - 5))

        def stat_z(n):
            st = stn[n % 3]
            ev["bn", "stn", n] = dve.do(lambda e: e.bn_stats(st[:, 0:6], z[n % 5][:]), ev["z", n],
                                        got("zn", n - 3))

        def norm_zn(n):
            st = stn[n % 3]
            ev["zn", n] = dve.do(lambda e: e.tensor_scalar(
                zn[n % 2][:], z[n % 5][:], st[:, 6:7], st[:, 8:9], ALU.subtract, ALU.mult),
                got("stn", n), got("znT", n - 2))

        def turn_zn(n):
            dst = bank[B_TURN]
            for k in range(KD):
                e = turn(dst[:, k * P:(k + 1) * P], zn[n % 2][:, k * P:(k + 1) * P], ev["zn", n],
                         last_read[B_TURN], signal=k == KD - 1)
            ev["znT", n] = e
            for k in range(KD):
                w, b = cols[:, C_LN + k:C_LN + k + 1], cols[:, C_LN + KD + k:C_LN + KD + k + 1]
                a = act.do(lambda e, k=k, w=w, b=b: e.activation(
                    xnt[0][:, k], dst[:, k * P:(k + 1) * P], ACT.Identity, bias=b, scale=w),
                    e, got("xnl", n - 1))
                a = act.do(lambda e, k=k, w=w, b=b: e.activation(
                    xnts[0][n % 2][:, k], dst[:, k * P:(k + 1) * P], ACT.Identity, bias=b, scale=w),
                    got("qkv", n - 2))
            ev["xnh", n] = last_read[B_TURN] = a

        def low_zn(n):
            ev["xnl", n] = dve.do(lambda e: e.tensor_tensor(
                xnts[1][n % 2][:], xnt[0][:], f32(xnts[0][n % 2][:]), ALU.subtract), ev["xnh", n],
                got("qkv", n - 2))

        def qkv(n):
            hi, lo = xnts[0][n % 2], xnts[1][n % 2]
            for b, c0, w in ((B_QK, 0, 2 * D), (B_V, 2 * D, D)):
                dst = bank[b][:, 0:w]
                add_bias(dst, bias_rows[:, c0:c0 + w], True, last_read[b], ev["xnl", n], ev["xnh", n])
                for k in range(KD):
                    e = product(dst, (hi[:, k], lo[:, k]),
                                (qkv_w[0][:, k, c0:c0 + w], qkv_w[1][:, k, c0:c0 + w]), False, k == KD - 1,
                                signal=k == KD - 1)
                ev["qkv", n] = e
                if b == B_QK:
                    e_qk = e
            a = act.do(lambda e: e.activation(soft[0][:], bank[B_QK][:], ACT.Relu, scale=-1.0), e_qk,
                       got("feat", n - 1))
            ev["soft", n] = act.do(lambda e: e.activation(soft[0][:], soft[0][:], ACT.Exp, scale=-1.0), a)
            ev["v", n] = last_read[B_V] = act.do(lambda e: e.copy(vals[n % 3][:], bank[B_V][:, 0:D]), e,
                                                 got("pv", n - 3), got("pvp", n - 3))

        def exp_table(n):
            ev["exp_table",] = act.do(lambda e: e.activation(scrap[:], minus_half[:, 0:1], ACT.Exp),
                                     got("exp_table"))

        def feat(n):
            ev["feat", n] = last_read[B_QK] = dve.do(lambda e: e.scalar_tensor_tensor(
                out=feats[n % 2][:], in0=bank[B_QK][:], scalar=0.0, in1=soft[0][:], op0=ALU.max, op1=ALU.add),
                ev["soft", n], got("pk", n - 2), got("pkp", n - 2))

        slot_of = [0]
        place_free = {}

        def products(n, kind, c, eng):
            i = slot_of[0] % 8
            slot_of[0] += 1
            dst = prod_[i][:].rearrange("p j (a b) -> p j a b", a=HEADS)
            wide = [P, 4, HEADS, HEADS]
            if kind == "k":
                f = feats[n % 2]
                left = f[:, 0:D].rearrange("p (h d) -> p d h", d=HD)[:, 4 * c:4 * c + 4]
                right = f[:, D:2 * D].rearrange("p (h d) -> p d h", d=HD)[:, 4 * c:4 * c + 4]
                need = ev["feat", n]
            else:
                left = score[n % 2][:].rearrange("p (h g) -> p g h", g=HEADS)[:, 4 * c:4 * c + 4]
                right = vals[n % 3][:].rearrange("p (g e) -> p g e", e=HD)[:, 4 * c:4 * c + 4]
                need = ev["score", n]
            left = left.unsqueeze(3).broadcast_to(wide)
            right = right.unsqueeze(2).broadcast_to(wide)
            e = eng.do(lambda e: e.tensor_tensor(dst, left, right, ALU.mult),
                                             need, ev["v", n], place_free.get(i))
            ev["p" + kind + ("p" if eng is pool else ""), n] = e
            ev.setdefault(("chunks" + kind, n), {})[c] = (i, e)

        def join(n, kind, eng, a, b):
            chunks = ev["chunks" + kind, n]
            (ia, ea), (ib, eb) = chunks[a], chunks.pop(b)
            e = eng.do(lambda e: e.tensor_tensor(prod_[ia][:], prod_[ia][:], prod_[ib][:], ALU.add), ea, eb)
            place_free[ib] = e
            del chunks[a]
            chunks[a] = (ia, e)

        def gather_products(n, kind):
            dst = bank[B_ACC]
            chunks = ev["chunks" + kind, n]
            for c, (i, e) in enumerate(chunks.values()):
                for j in range(4):
                    for half in range(KD):
                        first, last = c == 0 and j == 0, c == len(chunks) - 1 and j == 3
                        done = turn(dst[:, half * P:(half + 1) * P], prod_[i][:, j, half * P:(half + 1) * P], e,
                                    last_read[B_ACC], start=first and half == 0, stop=last,
                                    signal=j == 3 and half == KD - 1)
                place_free[i] = done
            return done

        def scores_t(n):
            e = gather_products(n, "k")
            ev["stt", n] = last_read[B_ACC] = act.do(lambda e: e.copy(stt[0][:], bank[B_ACC][:, 0:D]), e,
                                                     got("sback", n - 1))

        def scores_back(n):
            dst = bank[B_S]
            for k in range(KD):
                e = turn(dst[:, k * P:(k + 1) * P], stt[0][:, k * P:(k + 1) * P], ev["stt", n], last_read[B_S],
                         signal=k == KD - 1)
            ev["sback", n] = e

        def sum_scores(n, part):
            s, sm = bank[B_S][:, 0:D].rearrange("p (h g) -> p h g", g=HEADS), ssum[n % 2]
            if part == 0:
                e = dve.do(lambda e: e.tensor_reduce(sm[:, 0], s, AX, ALU.add), ev["sback", n])
            elif part == 1:
                e = dve.do(lambda e: e.tensor_scalar(sm[:, 0], sm[:, 0], ATTN_EPS, None, ALU.add), ev["ssum", n])
            else:
                e = dve.do(lambda e: e.reciprocal(sm[:, 1], sm[:, 0]), ev["ssum", n])
            ev["ssum", n] = e

        def scale_scores(n):
            s, sm = bank[B_S][:, 0:D].rearrange("p (h g) -> p h g", g=HEADS), ssum[n % 2]
            ev["score", n] = last_read[B_S] = dve.do(lambda e: e.tensor_tensor(
                score[n % 2][:].rearrange("p (h g) -> p h g", g=HEADS), s,
                sm[:, 1].unsqueeze(2).broadcast_to([P, HEADS, HEADS]), ALU.mult), ev["ssum", n],
                got("pv", n - 2), got("pvp", n - 2))

        def attended(n):
            e = gather_products(n, "v")
            a = act.do(lambda e: e.copy(ot[0][:], bank[B_ACC][:, 0:D]), e, got("otl", n - 1))
            ev["oth", n] = last_read[B_ACC] = act.do(lambda e: e.copy(ots[0][n % 2][:], bank[B_ACC][:, 0:D]),
                                                     got("wo", n - 2))

        def low_o(n):
            ev["otl", n] = dve.do(lambda e: e.tensor_tensor(
                ots[1][n % 2][:], ot[0][:], f32(ots[0][n % 2][:]), ALU.subtract), ev["oth", n], got("wo", n - 2))

        def project(n):
            dst = bank[B_V][:, 0:D]
            add_bias(dst, bias_rows[:, BO:BO + D], True, last_read[B_V], ev["otl", n])
            for k in range(KD):
                e = product(dst, (ots[0][n % 2][:, k * P:(k + 1) * P], ots[1][n % 2][:, k * P:(k + 1) * P]),
                            (o_w[0][:, k], o_w[1][:, k]), False, k == KD - 1, signal=k == KD - 1)
            ev["wo", n] = e

        def residual(n):
            e = ev["xa", n] = last_read[B_V] = dve.do(lambda e: e.tensor_tensor(
                xa[n % 3][:], bank[B_V][:, 0:D], z[n % 5][:], ALU.add), ev["wo", n], got("xr", n - 3),
                got("hn", n - 3), got("xr", n - 3))
            ev["xr", n] = pool.do(lambda e: e.tensor_tensor(xr[n % 10][:], x1[n % 8][:], xa[n % 3][:], ALU.add), e,
                                  got("x2", n - 10))

        def stat_h(n):
            st = sth[n % 3]
            ev["bn", "sth", n] = dve.do(lambda e: e.bn_stats(st[:, 0:6], xa[n % 3][:]), ev["xa", n],
                                        got("hn", n - 3))

        def norm_h(n):
            st = sth[n % 3]
            ev["hn", n] = dve.do(lambda e: e.tensor_scalar(
                hn[n % 2][:], xa[n % 3][:], st[:, 6:7], st[:, 8:9], ALU.subtract, ALU.mult), ev["sth", n],
                got("hnT", n - 2))

        def turn_h(n):
            g, t = divmod(n, GROUP)
            dst = bank[B_TURN]
            for k in range(KD):
                e = turn(dst[:, k * P:(k + 1) * P], hn[n % 2][:, k * P:(k + 1) * P], ev["hn", n],
                         last_read[B_TURN], signal=k == KD - 1)
            ev["hnT", n] = e
            for k in range(KD):
                w, b = (cols[:, C_LN + i * KD + k:C_LN + i * KD + k + 1] for i in (2, 3))
                a = act.do(lambda e, k=k, w=w, b=b: e.activation(
                    hnt[0][:, k], dst[:, k * P:(k + 1) * P], ACT.Identity, bias=b, scale=w), e, got("hnl", n - 1))
                a = act.do(lambda e, k=k, w=w, b=b: e.activation(
                    hnts[0][g % 2][:, k, t * P:(t + 1) * P], dst[:, k * P:(k + 1) * P], ACT.Identity, bias=b,
                    scale=w), got("up", g - 2, KM - 1))
            ev["hnh", n] = last_read[B_TURN] = a

        def low_h(n):
            g, t = divmod(n, GROUP)
            ev["hnl", n] = dve.do(lambda e: e.tensor_tensor(
                hnts[1][g % 2][:, :, t * P:(t + 1) * P], hnt[0][:], f32(hnts[0][g % 2][:, :, t * P:(t + 1) * P]),
                ALU.subtract), ev["hnh", n], got("up", g - 2, KM - 1))

        def up_mid(g, m):
            b, u = B_QK if g == NG - 1 and m % 2 else B_UP, g * KM + m
            dst = bank[b]
            for k in range(KD):
                e = product(dst[:], (up_w[0][:, k, m * P:(m + 1) * P], up_w[1][:, k, m * P:(m + 1) * P]),
                            (hnts[0][g % 2][:, k], hnts[1][g % 2][:, k]), k == 0, k == KD - 1,
                            ev["hnl", g * GROUP + GROUP - 1], last_read[b], signal=k == KD - 1)
            ev["up", g, m] = e
            bias = cols[:, C_FCB + m:C_FCB + m + 1]
            a = act.do(lambda e: e.activation(hid[u % 2][:], dst[:], ACT.Gelu, bias=bias), e, got("hl", u - 2))
            a = act.do(lambda e: e.activation(hids[0][u % 3][:], dst[:], ACT.Gelu, bias=bias), got("down", u - 3))
            ev["hh", u] = last_read[b] = a
            ev["hl", u] = pool.do(lambda e: e.tensor_tensor(
                hids[1][u % 3][:], hid[u % 2][:], f32(hids[0][u % 3][:]), ALU.subtract), a, got("down", u - 3))

        def down_mid(g, m):
            u = g * KM + m
            for t in range(GROUP):
                dst = bank[B_DOWN + t // 2][:, (t % 2) * D:(t % 2 + 1) * D]
                if m == 0:
                    add_bias(dst, bias_rows[:, PB:PB + D], t % 2 == 0, last_read[B_DOWN + t // 2])
                e = product(dst, (hids[0][u % 3][:, t * P:(t + 1) * P], hids[1][u % 3][:, t * P:(t + 1) * P]),
                            (down_w[0][:, m], down_w[1][:, m]), False, m == KM - 1, ev["hl", u], ev["hh", u],
                            signal=t == GROUP - 1)
            ev["down", u] = e

        def x2(g):
            for t in range(GROUP):
                n = g * GROUP + t
                src = bank[B_DOWN + t // 2][:, (t % 2) * D:(t % 2 + 1) * D]
                ev["x2", n] = last_read[B_DOWN + t // 2] = dve.do(lambda e, n=n, src=src: e.tensor_tensor(
                    rb.row(n), src, xr[n % 10][:], ALU.add), ev["down", g * KM + KM - 1],
                    ev["xr", n], rb.place_free(n), got("x2s", n - 2 * GROUP))
                ev["x2s", n] = sp.dma(r_store, lambda e, n=n: e.dma_start(
                    late_rows[n * P:(n + 1) * P, :], rb.row(n)), ev["x2", n])

        for n in range(2):
            load(n)
        attention_over = NT + 4
        for s in range(NT + 11):
            def on(k, f):
                if 0 <= s - k < NT:
                    f(s - k)

            def every(first, f):
                g, t = divmod(s - first, GROUP)
                if t == 0 and 0 <= g < NG:
                    f(g)

            g_up, j_up = divmod(s - 10, GROUP)
            g_down, j_down = divmod(s - 11, GROUP)
            units = []
            for first in (15, 16):
                every(first, lambda g: units.extend(g * GROUP + 2 * (first - 15) + i for i in range(2)))

            def turn_unit(n):
                last_read[B_TURN] = rb.turned(n, bank[B_TURN], last_read[B_TURN])

            def choose(g):
                last_read[B_S] = rb.choose(g)
                rb.soften(g)

            def dispatch(g):
                last_read[B_S] = rb.dispatch(g)

            def logits(i):
                every(17, lambda g: rb.logits(g * GROUP + i, bank[B_S], last_read[B_S]))

            on(-2, load)
            on(2, turn_zn)
            light = s < 10
            on(5, low_o)
            every(15, rb.roots)
            if 0 <= g_up < NG:
                up_mid(g_up, 2 * j_up)
            if 0 <= g_down < NG:
                down_mid(g_down, 2 * j_down + 1)
            on(4, lambda n: [products(n, "v", c, dve if c == 0 else pool) for c in (0, 3)])
            on(2, low_zn)
            on(5, project)
            every(18, lambda g: rb.count(g, bank[B_S], last_read[B_S]))
            logits(0)
            on(5, residual)
            every(15, rb.shifts)
            every(14, x2)
            for n in units:
                rb.normed(n)
            on(6, turn_h)
            logits(1)
            on(5, stat_h)
            every(18, dispatch)
            on(18, rb.send)
            on(5, lambda n: rstd(sth[n % 3], ("sth", n)))
            on(4, lambda n: [products(n, "v", c, pool if light and c == 2 else dve) for c in (1, 2)])
            if light:
                on(2, qkv)
            on(3, scores_t)
            logits(2)
            logits(3)
            on(2, exp_table)
            if not light:
                on(2, qkv)
            every(17, choose)
            on(1, norm_z)
            if light or s % 4 != 2:
                on(4, lambda n: join(n, "v", dve, 0, 1))
            on(1, stat_z)
            on(6, low_h)
            on(1, lambda n: rstd(stn[n % 3], ("stn", n)))
            for n in units[0:1] if s < NT + 2 else ():
                turn_unit(n)
            if 0 <= g_up < NG:
                up_mid(g_up, 2 * j_up + 1)
            on(3, scores_back)
            if 0 <= g_up < NG:
                down_mid(g_up, 2 * j_up)
            on(2, feat)
            on(5, norm_h)
            on(1, norm_zn)
            if light:
                on(2, lambda n: [products(n, "k", c, pool if c in (2, 3) else dve) for c in (0, 1, 2, 3)])
            else:
                on(2, lambda n: [products(n, "k", 2, dve), products(n, "k", 3, pool)])
                on(2, lambda n: join(n, "k", pool, 2, 3))
                on(2, lambda n: [products(n, "k", c, dve) for c in (0, 1)])
            on(3, lambda n: sum_scores(n, 0))
            on(0, stat_x)
            on(3, lambda n: sum_scores(n, 1))
            on(0, lambda n: rstd(stz[n % 3], ("stz", n)))
            on(3, lambda n: sum_scores(n, 2))
            on(3, scale_scores)
            for n in units[1:2] if s < NT + 2 else units:
                turn_unit(n)
            on(4, attended)
            every(14, lambda g: rb.stats(g, {n: ev["x2", n] for n in rb.tiles(g)}))
            if s == attention_over:
                bottom_free = so_far()
                sp.wait(*bottom_free)
                for c in range(KE // 2):
                    ex_b.load_weights(0, c)
            c = s - attention_over - 2
            if 0 <= c < KE // 2:
                for eng in (dve, act, pool):
                    eng.wait(*bottom_free)
                ex_b.split_weights(0, c, dve)
                ex_b.load_weights(1, c)

        g = NG - 1
        rb.roots(g)
        rb.shifts(g)
        for n in range(s - 18 + 1, NT - GROUP):
            rb.send(n)
        for n in rb.tiles(g):
            rb.normed(n)
        for n in rb.tiles(g):
            rb.turned(n, bank[(B_TURN, B_V, B_ACC, B_QK)[n % GROUP]], *last_read.values())
        for n in rb.tiles(g):
            rb.logits(n, bank[B_S], last_read[B_S])
        last_read[B_S] = rb.choose(g)
        rb.soften(g)
        rb.count(g, bank[B_S], last_read[B_S])
        rb.dispatch(g)
        for n in rb.tiles(g):
            rb.send(n)
        done_mid = everything()

        for s in (dve, act, pool, sp, pe):
            s.wait(*done_mid)
        ex_b.run(tables[1], late_rows, out_rows, done_mid, done_mid)

        sp.wait(*[v for r in rings for v in r.all()])

        block = ctx.enter_context(nc.Block())

        @block.sync
        def _(eng):
            sp.play(eng)

        @block.gpsimd
        def _(eng):
            pool.play(eng)

        @block.scalar
        def _(eng):
            act.play(eng)

        @block.vector
        def _(eng):
            dve.play(eng)

        @block.tensor
        def _(eng):
            pe.play(eng)


_INS = ["L0_attn_q_x", "L0_attn_ln1_w", "L0_attn_ln1_b", "L0_attn_wq", "L0_attn_bq", "L0_attn_wk", "L0_attn_bk",
        "L0_attn_wv", "L0_attn_bv", "L0_attn_wo", "L0_attn_bo", "L0_attn_ln2_w", "L0_attn_ln2_b", "L0_attn_fc_w",
        "L0_attn_fc_b", "L0_attn_proj_w", "L0_attn_proj_b", "L0_ffn_w_switch", "L0_ffn_b_switch", "L0_ffn_w1",
        "L0_ffn_b1", "L0_ffn_w2", "L0_ffn_b2"]
_OUTS = [((8, 512, 256), "float32")]


def kernel(**inputs):
    import numpy as _np
    import concourse.bacc as _bacc
    from concourse import mybir as _mybir
    from concourse.bass_utils import run_bass_kernel_spmd as _run

    nc = _bacc.Bacc("TRN2", target_bir_lowering=False, num_devices=1)
    arrays, args = {}, []
    for name in _INS:
        a = _np.ascontiguousarray(inputs[name])
        arrays[f"in_{name}_dram"] = a
        args.append(nc.dram_tensor(f"in_{name}_dram", a.shape, _mybir.dt.from_np(a.dtype), kind="ExternalInput").ap())
    for i, (shape, dtype) in enumerate(_OUTS):
        dt = _mybir.dt.from_np(_np.dtype(dtype))
        args.append(nc.dram_tensor(f"out_{i}_dram", shape, dt, kind="ExternalOutput").ap())
    build(nc, *args)
    r = _run(nc, [arrays], core_ids=[0])
    return r.results[0]["out_0_dram"]
```
